# Optimizing a Trainium2 kernel written in Bass

```python
import numpy as np
import jax
import jax.numpy as jnp

def _softmax(x, axis=-1):
    return jax.nn.softmax(x, axis=axis)

def _gelu(x):
    return jax.nn.gelu(x, approximate=True)

def _silu(x):
    return jax.nn.silu(x)

def _sigmoid(x):
    return jax.nn.sigmoid(x)

def _layernorm(x, axis=-1, eps=1e-05):
    m = jnp.mean(x, axis=axis, keepdims=True)
    v = jnp.var(x, axis=axis, keepdims=True)
    return (x - m) / jnp.sqrt(v + eps)

def _scatter_add(tgt, idx, src, axis=0):
    return tgt.at[idx].add(src)

def _segment_sum(src, seg, n):
    return jax.ops.segment_sum(src, seg, n)
kernel_name = 'mk_dlrm_tower_d1_rec_r8_e61041'

def setup_inputs(seed: int=0):
    np.random.seed(seed)
    _w = jnp.asarray

    def _rec_inputs():
        import jax
        import jax.numpy as jnp
        _tk = jax.random.key(seed)
        dense_ctx = jax.random.normal(jax.random.fold_in(_tk, 190), (512, 16), jnp.float32)
        ids = jnp.stack([jax.random.randint(jax.random.fold_in(_tk, 200 + f), (512,), 0, v, jnp.int32) for f, v in enumerate([1000, 1250, 1000, 125000, 1000, 1000, 125000, 12500, 1250, 1000, 12500, 125000, 1000, 12500, 12500, 12500, 12500, 1250, 1000, 1250, 1000, 1250, 125000, 1000, 1000, 1000, 1250, 12500, 12500, 12500, 1250, 125000])], axis=1)
        tbl_0 = 0.05 * jax.random.normal(jax.random.fold_in(_tk, 500 + 0), (1000, 16), jnp.float32)
        tbl_1 = 0.05 * jax.random.normal(jax.random.fold_in(_tk, 500 + 1), (1250, 16), jnp.float32)
        tbl_2 = 0.05 * jax.random.normal(jax.random.fold_in(_tk, 500 + 2), (1000, 16), jnp.float32)
        tbl_3 = 0.05 * jax.random.normal(jax.random.fold_in(_tk, 500 + 3), (125000, 16), jnp.float32)
        tbl_4 = 0.05 * jax.random.normal(jax.random.fold_in(_tk, 500 + 4), (1000, 16), jnp.float32)
        tbl_5 = 0.05 * jax.random.normal(jax.random.fold_in(_tk, 500 + 5), (1000, 16), jnp.float32)
        tbl_6 = 0.05 * jax.random.normal(jax.random.fold_in(_tk, 500 + 6), (125000, 16), jnp.float32)
        tbl_7 = 0.05 * jax.random.normal(jax.random.fold_in(_tk, 500 + 7), (12500, 16), jnp.float32)
        tbl_8 = 0.05 * jax.random.normal(jax.random.fold_in(_tk, 500 + 8), (1250, 16), jnp.float32)
        tbl_9 = 0.05 * jax.random.normal(jax.random.fold_in(_tk, 500 + 9), (1000, 16), jnp.float32)
        tbl_10 = 0.05 * jax.random.normal(jax.random.fold_in(_tk, 500 + 10), (12500, 16), jnp.float32)
        tbl_11 = 0.05 * jax.random.normal(jax.random.fold_in(_tk, 500 + 11), (125000, 16), jnp.float32)
        tbl_12 = 0.05 * jax.random.normal(jax.random.fold_in(_tk, 500 + 12), (1000, 16), jnp.float32)
        tbl_13 = 0.05 * jax.random.normal(jax.random.fold_in(_tk, 500 + 13), (12500, 16), jnp.float32)
        tbl_14 = 0.05 * jax.random.normal(jax.random.fold_in(_tk, 500 + 14), (12500, 16), jnp.float32)
        tbl_15 = 0.05 * jax.random.normal(jax.random.fold_in(_tk, 500 + 15), (12500, 16), jnp.float32)
        tbl_16 = 0.05 * jax.random.normal(jax.random.fold_in(_tk, 500 + 16), (12500, 16), jnp.float32)
        tbl_17 = 0.05 * jax.random.normal(jax.random.fold_in(_tk, 500 + 17), (1250, 16), jnp.float32)
        tbl_18 = 0.05 * jax.random.normal(jax.random.fold_in(_tk, 500 + 18), (1000, 16), jnp.float32)
        tbl_19 = 0.05 * jax.random.normal(jax.random.fold_in(_tk, 500 + 19), (1250, 16), jnp.float32)
        tbl_20 = 0.05 * jax.random.normal(jax.random.fold_in(_tk, 500 + 20), (1000, 16), jnp.float32)
        tbl_21 = 0.05 * jax.random.normal(jax.random.fold_in(_tk, 500 + 21), (1250, 16), jnp.float32)
        tbl_22 = 0.05 * jax.random.normal(jax.random.fold_in(_tk, 500 + 22), (125000, 16), jnp.float32)
        tbl_23 = 0.05 * jax.random.normal(jax.random.fold_in(_tk, 500 + 23), (1000, 16), jnp.float32)
        tbl_24 = 0.05 * jax.random.normal(jax.random.fold_in(_tk, 500 + 24), (1000, 16), jnp.float32)
        tbl_25 = 0.05 * jax.random.normal(jax.random.fold_in(_tk, 500 + 25), (1000, 16), jnp.float32)
        tbl_26 = 0.05 * jax.random.normal(jax.random.fold_in(_tk, 500 + 26), (1250, 16), jnp.float32)
        tbl_27 = 0.05 * jax.random.normal(jax.random.fold_in(_tk, 500 + 27), (12500, 16), jnp.float32)
        tbl_28 = 0.05 * jax.random.normal(jax.random.fold_in(_tk, 500 + 28), (12500, 16), jnp.float32)
        tbl_29 = 0.05 * jax.random.normal(jax.random.fold_in(_tk, 500 + 29), (12500, 16), jnp.float32)
        tbl_30 = 0.05 * jax.random.normal(jax.random.fold_in(_tk, 500 + 30), (1250, 16), jnp.float32)
        tbl_31 = 0.05 * jax.random.normal(jax.random.fold_in(_tk, 500 + 31), (125000, 16), jnp.float32)
        _rk = jax.random.fold_in(_tk, 7)
        W_top1 = 0.0606339 * jax.random.normal(jax.random.fold_in(_tk, 801), (272, 512), jnp.float32)
        W_top2 = 0.0441942 * jax.random.normal(jax.random.fold_in(_tk, 802), (512, 256), jnp.float32)
        W_top3 = 0.0625 * jax.random.normal(jax.random.fold_in(_tk, 803), (256, 1), jnp.float32)
        b_top1 = jnp.zeros((512,), jnp.float32)
        b_top2 = jnp.zeros((256,), jnp.float32)
        return (dense_ctx, ids, tbl_0, tbl_1, tbl_2, tbl_3, tbl_4, tbl_5, tbl_6, tbl_7, tbl_8, tbl_9, tbl_10, tbl_11, tbl_12, tbl_13, tbl_14, tbl_15, tbl_16, tbl_17, tbl_18, tbl_19, tbl_20, tbl_21, tbl_22, tbl_23, tbl_24, tbl_25, tbl_26, tbl_27, tbl_28, tbl_29, tbl_30, tbl_31, W_top1, b_top1, W_top2, b_top2, W_top3)
    dense_ctx, ids, tbl_0, tbl_1, tbl_2, tbl_3, tbl_4, tbl_5, tbl_6, tbl_7, tbl_8, tbl_9, tbl_10, tbl_11, tbl_12, tbl_13, tbl_14, tbl_15, tbl_16, tbl_17, tbl_18, tbl_19, tbl_20, tbl_21, tbl_22, tbl_23, tbl_24, tbl_25, tbl_26, tbl_27, tbl_28, tbl_29, tbl_30, tbl_31, W_top1, b_top1, W_top2, b_top2, W_top3 = _rec_inputs()

    def _L0_rec_setup():
        import jax, jax.numpy as jnp
        import numpy as np
        NUM_FIELDS = 32
        EMBED_DIM = 16
        BATCH = 512
        CROSS_SIZES = [128, 128, 128]

        def _cin_forward(x, Ws, bs):
            x0 = x
            h = x
            xs = []
            n_layers = len(Ws)
            for i in range(n_layers):
                B, F, E = x0.shape
                G = h.shape[1]
                z = (x0[:, :, None, :] * h[:, None, :, :]).reshape(B, F * G, E)
                y = jax.nn.relu(jnp.einsum('oc,bce->boe', Ws[i], z) + bs[i][None, :, None])
                if i != n_layers - 1:
                    half = y.shape[1] // 2
                    x_keep, h = (y[:, :half, :], y[:, half:, :])
                else:
                    x_keep, h = (y, y)
                xs.append(x_keep)
            return jnp.sum(jnp.concatenate(xs, axis=1), axis=2)
        key = jax.random.key(seed)
        ks = jax.random.split(key, 8)
        x = jax.random.normal(ks[0], (BATCH, NUM_FIELDS, EMBED_DIM), dtype=jnp.float32)
        prev = NUM_FIELDS
        inp = {'x': x}
        for i, cs in enumerate(CROSS_SIZES):
            in_ch = NUM_FIELDS * prev
            scale = 1.0 / np.sqrt(in_ch)
            inp[f'W{i}'] = jax.random.uniform(ks[1 + 2 * i], (cs, in_ch), dtype=jnp.float32, minval=-scale, maxval=scale)
            inp[f'b{i}'] = jax.random.uniform(ks[2 + 2 * i], (cs,), dtype=jnp.float32, minval=-scale, maxval=scale)
            prev = cs // 2
        return inp
    _L0_rec_all = _L0_rec_setup()
    _L0_rec_in = {k: v for k, v in _L0_rec_all.items() if k in ('W0', 'b0', 'W1', 'b1', 'W2', 'b2')}
    del _L0_rec_all
    return {'dense_ctx': dense_ctx, 'ids': ids, 'tbl_0': tbl_0, 'tbl_1': tbl_1, 'tbl_2': tbl_2, 'tbl_3': tbl_3, 'tbl_4': tbl_4, 'tbl_5': tbl_5, 'tbl_6': tbl_6, 'tbl_7': tbl_7, 'tbl_8': tbl_8, 'tbl_9': tbl_9, 'tbl_10': tbl_10, 'tbl_11': tbl_11, 'tbl_12': tbl_12, 'tbl_13': tbl_13, 'tbl_14': tbl_14, 'tbl_15': tbl_15, 'tbl_16': tbl_16, 'tbl_17': tbl_17, 'tbl_18': tbl_18, 'tbl_19': tbl_19, 'tbl_20': tbl_20, 'tbl_21': tbl_21, 'tbl_22': tbl_22, 'tbl_23': tbl_23, 'tbl_24': tbl_24, 'tbl_25': tbl_25, 'tbl_26': tbl_26, 'tbl_27': tbl_27, 'tbl_28': tbl_28, 'tbl_29': tbl_29, 'tbl_30': tbl_30, 'tbl_31': tbl_31, 'W_top1': W_top1, 'b_top1': b_top1, 'W_top2': W_top2, 'b_top2': b_top2, 'W_top3': W_top3, 'L0_rec_W0': _L0_rec_in['W0'], 'L0_rec_b0': _L0_rec_in['b0'], 'L0_rec_W1': _L0_rec_in['W1'], 'L0_rec_b1': _L0_rec_in['b1'], 'L0_rec_W2': _L0_rec_in['W2'], 'L0_rec_b2': _L0_rec_in['b2']}

def reference(dense_ctx, ids, tbl_0, tbl_1, tbl_2, tbl_3, tbl_4, tbl_5, tbl_6, tbl_7, tbl_8, tbl_9, tbl_10, tbl_11, tbl_12, tbl_13, tbl_14, tbl_15, tbl_16, tbl_17, tbl_18, tbl_19, tbl_20, tbl_21, tbl_22, tbl_23, tbl_24, tbl_25, tbl_26, tbl_27, tbl_28, tbl_29, tbl_30, tbl_31, W_top1, b_top1, W_top2, b_top2, W_top3, L0_rec_W0, L0_rec_b0, L0_rec_W1, L0_rec_b1, L0_rec_W2, L0_rec_b2):
    import jax
    import jax.numpy as jnp

    def _L0_rec_ref(x, W0, b0, W1, b1, W2, b2):
        import jax, jax.numpy as jnp
        import numpy as np
        NUM_FIELDS = 32
        EMBED_DIM = 16
        BATCH = 512
        CROSS_SIZES = [128, 128, 128]

        def _cin_forward(x, Ws, bs):
            x0 = x
            h = x
            xs = []
            n_layers = len(Ws)
            for i in range(n_layers):
                B, F, E = x0.shape
                G = h.shape[1]
                z = (x0[:, :, None, :] * h[:, None, :, :]).reshape(B, F * G, E)
                y = jax.nn.relu(jnp.einsum('oc,bce->boe', Ws[i], z) + bs[i][None, :, None])
                if i != n_layers - 1:
                    half = y.shape[1] // 2
                    x_keep, h = (y[:, :half, :], y[:, half:, :])
                else:
                    x_keep, h = (y, y)
                xs.append(x_keep)
            return jnp.sum(jnp.concatenate(xs, axis=1), axis=2)
        return _cin_forward(x, [W0, W1, W2], [b0, b1, b2])
    e = jnp.stack([tbl_0[ids[:, 0]], tbl_1[ids[:, 1]], tbl_2[ids[:, 2]], tbl_3[ids[:, 3]], tbl_4[ids[:, 4]], tbl_5[ids[:, 5]], tbl_6[ids[:, 6]], tbl_7[ids[:, 7]], tbl_8[ids[:, 8]], tbl_9[ids[:, 9]], tbl_10[ids[:, 10]], tbl_11[ids[:, 11]], tbl_12[ids[:, 12]], tbl_13[ids[:, 13]], tbl_14[ids[:, 14]], tbl_15[ids[:, 15]], tbl_16[ids[:, 16]], tbl_17[ids[:, 17]], tbl_18[ids[:, 18]], tbl_19[ids[:, 19]], tbl_20[ids[:, 20]], tbl_21[ids[:, 21]], tbl_22[ids[:, 22]], tbl_23[ids[:, 23]], tbl_24[ids[:, 24]], tbl_25[ids[:, 25]], tbl_26[ids[:, 26]], tbl_27[ids[:, 27]], tbl_28[ids[:, 28]], tbl_29[ids[:, 29]], tbl_30[ids[:, 30]], tbl_31[ids[:, 31]]], axis=1)
    z = _L0_rec_ref(e, L0_rec_W0, L0_rec_b0, L0_rec_W1, L0_rec_b1, L0_rec_W2, L0_rec_b2)
    z = z.reshape(z.shape[0], -1)
    h = jnp.concatenate([z, dense_ctx], axis=1)
    h = jnp.maximum(h @ W_top1 + b_top1, 0.0)
    h = jnp.maximum(h @ W_top2 + b_top2, 0.0)
    y = h @ W_top3
    return y

_drawn_inputs = setup_inputs


def setup_inputs(seed=0):
    import zlib

    import numpy as np

    out = dict(_drawn_inputs(seed))
    spreads = {'b_top1': (0.0, 0.352), 'b_top2': (0.0, 0.395)}
    factors = {'tbl_0': 8.0,
     'tbl_1': 8.0,
     'tbl_2': 8.0,
     'tbl_3': 8.0,
     'tbl_4': 8.0,
     'tbl_5': 8.0,
     'tbl_6': 8.0,
     'tbl_7': 8.0,
     'tbl_8': 8.0,
     'tbl_9': 8.0,
     'tbl_10': 8.0,
     'tbl_11': 8.0,
     'tbl_12': 8.0,
     'tbl_13': 8.0,
     'tbl_14': 8.0,
     'tbl_15': 8.0,
     'tbl_16': 8.0,
     'tbl_17': 8.0,
     'tbl_18': 8.0,
     'tbl_19': 8.0,
     'tbl_20': 8.0,
     'tbl_21': 8.0,
     'tbl_22': 8.0,
     'tbl_23': 8.0,
     'tbl_24': 8.0,
     'tbl_25': 8.0,
     'tbl_26': 8.0,
     'tbl_27': 8.0,
     'tbl_28': 8.0,
     'tbl_29': 8.0,
     'tbl_30': 8.0,
     'tbl_31': 8.0,
     'L0_rec_W0': 8.0,
     'L0_rec_W1': 8.0,
     'L0_rec_W2': 8.0,
     'L0_rec_b0': 4.727,
     'L0_rec_b1': 7.087,
     'L0_rec_b2': 7.111}
    for name, (base, spread) in spreads.items():
        noise = np.random.default_rng([zlib.crc32(name.encode()), seed]).standard_normal(out[name].shape)
        drawn = base * np.exp(spread * noise) if base else spread * noise
        out[name] = jnp.asarray(drawn.astype(out[name].dtype))
    for name, factor in factors.items():
        out[name] = (out[name] * factor).astype(out[name].dtype)
    return out
```

```python
from contextlib import ExitStack

import concourse.bass as bass
from concourse import mybir

P = 128
FIELDS, EMBED, BATCH = 32, 16, 512
HALF = 64
ROWS = 32
CHUNKS = BATCH // ROWS
N = ROWS * EMBED
GATHERS = FIELDS * ROWS // P
GROUP = 4
TILES = FIELDS * HALF // P
GROUPS = TILES // GROUP
ROT = FIELDS // 2

Z_SLOTS, PAIR_SLOTS = 3, 5
W_LOTS = 2 + 2 * GROUPS
X0_LOADS, SMALL, TOPS = GROUP + 2, 2, 3
STEPS, SPLITS, POOLED = 2 * GROUPS + 1, 2 * GROUPS + 2, 2 * GROUPS
FIRST = 2
TURNS = (CHUNKS - 4 - FIRST + 1) // 2

F32 = mybir.dt.float32
F32R = mybir.dt.float32r
I32 = mybir.dt.int32
U32 = mybir.dt.uint32
ALU = mybir.AluOpType
ACT = mybir.ActivationFunctionType
AX = mybir.AxisListType

assert N == 512 and TILES == 16 and GROUPS == 4 and STEPS % Z_SLOTS == 0 and SPLITS % PAIR_SLOTS == 0


def steps(c):
    layers = [1] * (c < CHUNKS) + [0] * (c + 1 < CHUNKS) + [2] * (c >= 1)
    if c == 0:
        g, s, p = 1, 2, 0
    elif c < CHUNKS:
        g, s, p = STEPS * c - 3, SPLITS * c - 2, POOLED * c - 4
    else:
        g, s, p = STEPS * c - 4, SPLITS * c - 4, POOLED * c - 4
    out = []
    for layer in layers:
        for k in range(1 if layer == 0 else GROUPS):
            out.append((layer, k, g, s, p))
            g, s, p = g + 1, s + (2 if layer == 0 else 1), p + (layer != 0)
    return out


def pairs_through(g):
    last = STEPS * (CHUNKS - 1) - 3
    if g < 3:
        return 2 + g
    if g < last:
        c, k = divmod(g + 3, STEPS)
        return SPLITS * c - 2 + k + 1 + (k >= GROUPS)
    return SPLITS * (CHUNKS - 1) - 2 + g - last + 1


def split_weights(u):
    return (0, GROUP, 0) if u == 0 else (GROUP + 2 * (u - 2), 2, 2 * P)


def flat(tiles):
    return tiles.rearrange("p t o -> p (t o)")


def dlrm_tower(nc, idx_in, row0_in, ident_in, signs_in, columns_in, table, dense, w_cin, w_top1, w_top2, out):
    with ExitStack() as ctx:
        def sb(name, shape, dt=F32):
            return ctx.enter_context(nc.sbuf_tensor(name, shape, dt))

        def psum(name):
            return ctx.enter_context(nc.psum_tensor(name, [P, N], F32))

        def sem(name):
            return ctx.enter_context(nc.semaphore(name))

        x_dram = nc.dram_tensor("x_scratch", (2, 2 * FIELDS, N), F32, kind="Internal").ap()

        idx = sb("idx", [P, CHUNKS * GATHERS], I32)
        row0 = sb("row0", [P, CHUNKS * GATHERS], I32)
        rows_all = sb("rows_all", [P, CHUNKS * GATHERS], I32)
        rows_now = sb("rows_now", [P, 2, GATHERS], I32)
        ident = sb("ident", [P, P])
        signs = sb("signs", [P, 2])
        gathered = sb("gathered", [P, 2, GATHERS, EMBED])
        x_t = sb("x_t", [P, P])
        x_pair = sb("x_pair", [P, 2, TILES, N])
        x_rep = sb("x_rep", [P, N])
        x_rot = sb("x_rot", [P, GROUP, N])
        x_half = sb("x_half", [P, N])
        z = sb("z", [P, Z_SLOTS, GROUP, N])
        z_high = sb("z_high", [P, PAIR_SLOTS, 2, N], F32R)
        z_low = sb("z_low", [P, PAIR_SLOTS, 2, N], F32R)
        zl_full = sb("zl_full", [P, N])
        zl_high = sb("zl_high", [P, N], F32R)
        zl_parts = sb("zl_parts", [P, N], F32R)
        w_sym = sb("w_sym", [P, GROUP + 1, FIELDS, GROUP])
        w_direct = sb("w_direct", [P, TILES, P])
        w_high = sb("w_high", [P, GROUP + TILES, P], F32R)
        w_low = sb("w_low", [P, GROUP + TILES, P], F32R)
        wl_high = sb("wl_high", [P, P], F32R)
        wl_parts = sb("wl_parts", [P, P], F32R)
        columns = sb("columns", [P, 11])
        bias, bt1, bt2, wt3 = columns[:, 0:3], columns[:, 3:7], columns[:, 7:9], columns[:, 9:11]
        kept01 = sb("kept01", [P, 2, N])
        kept2 = sb("kept2", [P, N])
        sum01 = sb("sum01", [P, BATCH])
        sum2 = sb("sum2", [P, BATCH])
        dense_rows = sb("dense_rows", [P, BATCH // P, EMBED])
        dense_t = sb("dense_t", [EMBED, BATCH])
        wt1 = sb("wt1", [P, 2, 512])
        wt1_dense = sb("wt1_dense", [EMBED, 512])
        wt2 = sb("wt2", [P, 4, 256])
        result = sb("result", [1, BATCH])

        hid1 = x_pair[:, 0, 0:4, :]
        hid2 = x_pair[:, 0, 4:6, :]
        w_raw = [x_pair[:, 1, 4 * i:4 * i + 4, :].rearrange("p t n -> p (t n)") for i in range(4)]
        w0_wide = w_raw[2].rearrange("p (f g) -> p f g", f=FIELDS)
        w0_tall = w_raw[3].rearrange("p (f g) -> p f g", g=FIELDS)

        acc0, acc1, acc2 = psum("acc0"), psum("acc1"), psum("acc2")
        h1 = psum("h1")
        h2 = [psum("h2_even"), psum("h2_odd")]
        x_bank = psum("x_bank")
        spare = psum("spare")
        w_bank = [spare, h2[1]]
        top_bank = [h1, h2[0], x_bank, spare]

        idx_here, w0_here, w1_here, w2_here = sem("idx_here"), sem("w0_here"), sem("w1_here"), sem("w2_here")
        ident_here, small_here, top_here = sem("ident_here"), sem("small_here"), sem("top_here")
        wide_made = sem("wide_made")
        rows_made, rows_copied = sem("rows_made"), sem("rows_copied")
        sym_made, w_turned, w_rounded, w_ready = sem("sym_made"), sem("w_turned"), sem("w_rounded"), sem("w_ready")
        w_copied = sem("w_copied")
        dense_here, dense_turned, dense_ready = sem("dense_here"), sem("dense_turned"), sem("dense_ready")
        gather_done = [sem("gather_even"), sem("gather_odd")]
        x_turned, x_copied, x_stored, x0_here = sem("x_turned"), sem("x_copied"), sem("x_stored"), sem("x0_here")
        xp_here = [[sem(f"xp_here_{b}_{k}") for k in range(GROUPS)] for b in range(2)]
        z_made, last_made = sem("z_made"), sem("last_made")
        high_made, last_high = sem("high_made"), sem("last_high")
        low_dve, low_pool, last_parts = sem("low_dve"), sem("low_pool"), sem("last_parts")
        pairs_used = sem("pairs_used")
        h1_ready, h2_ready = sem("h1_ready"), sem("h2_ready")
        kept0_out, kept1_out, kept2_out = sem("kept0_out"), sem("kept1_out"), sem("kept2_out")
        sum01_made, sum2_made = sem("sum01_made"), sem("sum2_made")
        top1_done, hid1_ready = sem("top1_done"), sem("hid1_ready")
        top2_done, hid2_ready, top3_done = sem("top2_done"), sem("hid2_ready"), sem("top3_done")
        result_ready, out_stored = sem("result_ready"), sem("out_stored")

        def at(first, per_iteration, turn):
            return first if turn is None else first + turn * (2 * per_iteration)

        def all_iterations(eng, iteration):
            for c in range(FIRST):
                iteration(c, None)
            with eng.Fori(0, TURNS) as turn:
                iteration(FIRST, turn)
                iteration(FIRST + 1, turn)
            for c in range(FIRST + 2 * TURNS, CHUNKS + 1):
                iteration(c, None)

        block = ctx.enter_context(nc.Block())

        @block.sync
        def _(sp):
            sp.dma_start(idx[:], idx_in).then_inc(idx_here, 16)
            sp.dma_start(row0[:], row0_in).then_inc(idx_here, 16)
            w0 = w_cin[0].rearrange("o (f g) -> o f g", g=FIELDS)
            for half in range(2):
                sp.dma_start(w0_tall[:, half * FIELDS:(half + 1) * FIELDS, :], w0).then_inc(w0_here, 16)
            sp.dma_start(w_raw[0], w_cin[1]).then_inc(w1_here, 16)
            sp.dma_start(w_raw[1], w_cin[2]).then_inc(w2_here, 16)

            def store_x(c, turn):
                sp.wait_ge(x_copied, at(c + 1, 1, turn))
                for half in range(2):
                    rows = x_dram[c % 2, half * FIELDS:(half + 1) * FIELDS, :]
                    sp.dma_start(rows.rearrange("(q j) (e b) -> (j e) q b", j=GATHERS, b=ROWS),
                                 x_t[:].rearrange("p (q b) -> p q b", b=ROWS)).then_inc(x_stored, 16)

            def load_x0(c, turn):
                sp.wait_ge(x_stored, at(32 * (c + 1), 32, turn))
                x = x_dram[c % 2]
                wide = [FIELDS, GROUP, N]
                sp.dma_start(x_rep[:], x[0:FIELDS].unsqueeze(1).to_broadcast(wide)).then_inc(x0_here, 16)
                for j in range(GROUP):
                    rotated = bass.AP(x.tensor, x.offset + GROUP * j * N, [[N, FIELDS], [N, GROUP], [1, N]])
                    sp.dma_start(x_rot[:, j, :], rotated).then_inc(x0_here, 16)
                sp.dma_start(x_half[:], x[ROT:ROT + FIELDS].unsqueeze(1).to_broadcast(wide)).then_inc(x0_here, 16)

            def load_pair(c, k):
                src = x_dram[c % 2, 2 * GROUP * k:2 * GROUP * (k + 1), :].rearrange("(t a) n -> a t n", a=2)
                for a in range(2):
                    sp.dma_start(x_pair[HALF * a:HALF * (a + 1), c % 2, GROUP * k:GROUP * (k + 1), :],
                                 src[a:a + 1].to_broadcast([HALF, GROUP, N])).then_inc(xp_here[c % 2][k], 16)

            store_x(0, None)
            load_x0(0, None)
            for k in range(GROUPS):
                load_pair(0, k)
            store_x(1, None)
            load_x0(1, None)
            sp.wait_ge(w_turned, W_LOTS)
            for k in range(GROUPS):
                load_pair(1, k)

            def iteration(c, turn):
                used = {k: g + 1 for layer, k, g, _, _ in steps(c) if layer == 2}
                if c + 2 < CHUNKS:
                    store_x(c + 2, turn)
                for k in range(GROUPS):
                    if k == 2 and c + 2 < CHUNKS:
                        load_x0(c + 2, turn)
                    if c and c + 1 < CHUNKS:
                        sp.wait_ge(z_made, at(used[k], STEPS, turn))
                        load_pair(c + 1, k)

            all_iterations(sp, iteration)
            sp.wait_ge(result_ready, 1)
            sp.dma_start(out.rearrange("b o -> o b"), result[:]).then_inc(out_stored, 16)
            sp.wait_ge(out_stored, 16)

        @block.gpsimd
        def _(pool):
            def copy_rows(c, turn):
                first = c * GATHERS if turn is None else turn * (2 * GATHERS) + c * GATHERS
                nc.gpsimd.tensor_copy(rows_now[:, c % 2, :],
                                      rows_all[:, bass.ds(first, GATHERS)]).then_inc(rows_copied, 1)
                pool.wait_ge(rows_copied, at(c + 1, 1, turn))

            def gather(c, j):
                pool.indirect_dma_start(
                    gathered[:, c % 2, j, :], None, table,
                    bass.IndirectOffsetOnAxis(ap=rows_now[:, c % 2, j:j + 1].bitcast(U32), axis=0),
                ).then_inc(gather_done[c % 2], 16)

            pool.wait_ge(rows_made, 1)
            for c in range(3):
                if c == 2:
                    pool.wait_ge(x_turned, 1)
                copy_rows(c, None)
                for j in range(GATHERS):
                    gather(c, j)

            def iteration(c, turn):
                split = [(g, s) for layer, _, g, s, _ in steps(c) if layer]
                if c + 3 < CHUNKS:
                    pool.wait_ge(x_turned, at(c + 2, 1, turn))
                    copy_rows(c + 3, turn)
                for n, (g, s) in enumerate(split):
                    pool.wait_ge(high_made, at(s + 1, SPLITS, turn))
                    nc.gpsimd.tensor_tensor(z_low[:, s % PAIR_SLOTS], z[:, g % Z_SLOTS, 2:4],
                                            z_high[:, s % PAIR_SLOTS].bitcast(F32), ALU.subtract).then_inc(low_pool, 1)
                    if c + 3 < CHUNKS:
                        for j in range(n * GATHERS // len(split), (n + 1) * GATHERS // len(split)):
                            gather(c + 3, j)

            all_iterations(pool, iteration)

        @block.vector
        def _(dve):
            dve.wait_ge(idx_here, 32)
            nc.vector.tensor_tensor(rows_all[:], idx[:], row0[:], ALU.add).then_inc(rows_made, 1)

            def diagonals(raw, first, dims):
                return bass.AP(raw.tensor, raw.offset + first, [list(raw.ap[0])] + dims)

            wide, tall = 2 * FIELDS, FIELDS
            nc.vector.memset(w_sym[:, GROUP], 0.0).then_inc(sym_made, 1)
            dve.wait_ge(wide_made, 2)
            nc.vector.tensor_tensor(
                w_sym[:, 0:GROUP],
                diagonals(w0_wide, 0, [[GROUP, GROUP], [wide + 1, FIELDS], [1, GROUP]]),
                diagonals(w0_tall, 0, [[GROUP * tall, GROUP], [tall + 1, FIELDS], [tall, GROUP]]),
                ALU.add).then_inc(sym_made, 1)
            dve.wait_ge(sym_made, 2)
            nc.vector.tensor_copy(w_sym[:, 0, :, 0], diagonals(w0_wide, 0, [[wide + 1, FIELDS]])).then_inc(sym_made, 1)
            nc.vector.tensor_tensor(
                w_sym[:, GROUP, 0:ROT, 0:3],
                diagonals(w0_wide, ROT, [[wide + 1, ROT], [0, 3]]),
                diagonals(w0_tall, ROT * tall, [[tall + 1, ROT], [0, 3]]),
                ALU.add).then_inc(sym_made, 1)

            dve.wait_ge(small_here, 16 * SMALL)
            for u in range(W_LOTS):
                dve.wait_ge(w_rounded, u + 1)
                if u == 1:
                    op = nc.vector.scalar_tensor_tensor(out=wl_parts[:], in0=wl_high[:].bitcast(F32),
                                                        scalar=signs[:, 1:2], in1=w_bank[1][:, 0:P],
                                                        op0=ALU.mult, op1=ALU.add)
                else:
                    first, n, column = split_weights(u)
                    op = nc.vector.tensor_tensor(flat(w_low[:, first:first + n]), w_bank[u % 2][:, column:],
                                                 flat(w_high[:, first:first + n]).bitcast(F32), ALU.subtract)
                op.then_inc(w_ready, 1)
            dve.wait_ge(dense_turned, 1)
            nc.vector.tensor_copy(dense_t[:], w_bank[0][0:EMBED, :]).then_inc(dense_ready, 1)

            def layer0_products(chunk, g, turn):
                dve.wait_ge(x0_here, at(X0_LOADS * 16 * (chunk + 1), X0_LOADS * 16, turn))
                nc.vector.tensor_tensor(z[:, g % Z_SLOTS], x_rep[:].unsqueeze(1).to_broadcast([P, GROUP, N]),
                                        x_rot[:], ALU.mult).then_inc(z_made, 1)
                nc.vector.tensor_tensor(zl_full[:], x_rep[:], x_half[:], ALU.mult).then_inc(last_made, 1)

            def layer0_low(chunk, g, s, turn):
                for pair in range(2):
                    dve.wait_ge(high_made, at(s + pair + 1, SPLITS, turn))
                    nc.vector.tensor_tensor(z_low[:, (s + pair) % PAIR_SLOTS], z[:, g % Z_SLOTS, 2 * pair:2 * pair + 2],
                                            z_high[:, (s + pair) % PAIR_SLOTS].bitcast(F32),
                                            ALU.subtract).then_inc(low_dve, 1)
                dve.wait_ge(last_high, at(chunk + 1, 1, turn))
                nc.vector.scalar_tensor_tensor(out=zl_parts[:], in0=zl_high[:].bitcast(F32), scalar=signs[:, 0:1],
                                               in1=zl_full[:], op0=ALU.mult, op1=ALU.add).then_inc(last_parts, 1)

            def hidden_products(layer, chunk, k, g, turn):
                if layer == 1:
                    dve.wait_ge(xp_here[chunk % 2][k], at(32 * (chunk // 2 + 1), 16, turn))
                if k == 0:
                    dve.wait_ge(h1_ready if layer == 1 else h2_ready, at(chunk + 1, 1, turn))
                h = h1 if layer == 1 else h2[chunk % 2]
                nc.vector.tensor_tensor(z[:, g % Z_SLOTS], h[:].unsqueeze(1).to_broadcast([P, GROUP, N]),
                                        x_pair[:, chunk % 2, GROUP * k:GROUP * (k + 1), :],
                                        ALU.mult).then_inc(z_made, 1)

            def sum_components(chunk, turn, kept, total, ready, made):
                dve.wait_ge(ready, at(chunk + 1, 1, turn))
                first = chunk * ROWS if turn is None else turn * (2 * ROWS) + chunk * ROWS
                nc.vector.tensor_reduce(total[:, bass.ds(first, ROWS)], kept.rearrange("p (e b) -> p b e", b=ROWS),
                                        AX.X, ALU.add).then_inc(made, 1)

            def iteration(c, turn):
                todo = steps(c)
                behind = None
                for n, (layer, k, g, s, _) in enumerate(todo):
                    if g >= Z_SLOTS:
                        dve.wait_ge(pairs_used, at(pairs_through(g - Z_SLOTS), SPLITS, turn))
                    if layer == 0:
                        layer0_products(c + 1, g, turn)
                        behind = g, s
                    else:
                        hidden_products(layer, c + 1 - layer, k, g, turn)
                    if behind and (layer or n + 1 == len(todo)):
                        layer0_low(c + 1, *behind, turn)
                        behind = None
                    if n == 1 and c >= 1:
                        sum_components(c - 1, turn, kept01[:, (c - 1) % 2], sum01, kept1_out, sum01_made)
                    if n == min(GROUPS, len(todo) - 1) and c >= 2:
                        sum_components(c - 2, turn, kept2[:], sum2, kept2_out, sum2_made)

            layer0_products(0, 0, None)
            layer0_low(0, 0, 0, None)
            all_iterations(dve, iteration)
            sum_components(CHUNKS - 1, None, kept2[:], sum2, kept2_out, sum2_made)
            dve.wait_ge(top3_done, 1)
            nc.vector.tensor_copy(result[:], acc2[0:1, :]).then_inc(result_ready, 1)

        @block.scalar
        def _(act):
            act.dma_start(ident[:], ident_in).then_inc(ident_here, 16)
            smalls = [(signs[:], signs_in), (columns[:], columns_in)]
            assert len(smalls) == SMALL
            for dst, src in smalls:
                act.dma_start(dst, src).then_inc(small_here, 16)
            act.dma_start(dense_rows[:], dense.rearrange("(t p) e -> p t e", p=P)).then_inc(dense_here, 16)

            act.wait_ge(w0_here, 32)
            for half in range(2):
                nc.scalar.activation(w0_wide[:, :, half * FIELDS:(half + 1) * FIELDS], w0_tall[:, 0:FIELDS, :],
                                     ACT.Copy).then_inc(wide_made, 1)

            for u in range(W_LOTS):
                act.wait_ge(w_turned, u + 1)
                if u == 1:
                    op = nc.scalar.activation(wl_high[:], w_bank[1][:, 0:P], ACT.Copy)
                else:
                    first, n, column = split_weights(u)
                    if column:
                        nc.scalar.activation(flat(w_direct[:, 2 * (u - 2):2 * (u - 1)]), w_bank[u % 2][:, 0:column],
                                             ACT.Copy).then_inc(w_copied, 1)
                    op = nc.scalar.activation(flat(w_high[:, first:first + n]), w_bank[u % 2][:, column:], ACT.Copy)
                op.then_inc(w_rounded, 1)

            def copy_x(c, turn):
                act.wait_ge(x_turned, at(c + 1, 1, turn))
                if c:
                    act.wait_ge(x_stored, at(32 * c, 32, turn))
                nc.scalar.activation(x_t[:], x_bank[:, 0:P], ACT.Copy).then_inc(x_copied, 1)

            def round_pair(g, s, first, turn):
                act.wait_ge(z_made, at(g + 1, STEPS, turn))
                if s >= PAIR_SLOTS:
                    act.wait_ge(pairs_used, at(s - PAIR_SLOTS + 1, SPLITS, turn))
                nc.scalar.activation(z_high[:, s % PAIR_SLOTS], z[:, g % Z_SLOTS, first:first + 2],
                                     ACT.Copy).then_inc(high_made, 1)

            def round_layer0(chunk, g, s, turn):
                round_pair(g, s, 0, turn)
                round_pair(g, s + 1, 2, turn)
                act.wait_ge(last_made, at(chunk + 1, 1, turn))
                nc.scalar.activation(zl_high[:], zl_full[:], ACT.Copy).then_inc(last_high, 1)

            def relu(dst, acc, layer, half=None):
                rows = slice(None) if half is None else slice(HALF * half, HALF * (half + 1))
                return nc.scalar.activation(dst, acc[rows, :], ACT.Relu, bias=bias[rows, layer:layer + 1])

            def layer_out(layer, chunk, pairs, turn):
                act.wait_ge(pairs_used, at(pairs, SPLITS, turn))
                if layer == 2:
                    relu(kept2[:], acc2, 2).then_inc(kept2_out, 1)
                    return
                acc, h, ready, out_sem = ((acc0, h1, h1_ready, kept0_out),
                                          (acc1, h2[chunk % 2], h2_ready, kept1_out))[layer]
                relu(h[0:HALF, :], acc, layer, 1)
                relu(h[HALF:P, :], acc, layer, 1).then_inc(ready, 1)
                relu(kept01[HALF * layer:HALF * (layer + 1), chunk % 2], acc, layer, 0).then_inc(out_sem, 1)

            def iteration(c, turn):
                todo = steps(c)
                ends = {layer: s + (2 if layer == 0 else 1) for layer, _, _, s, _ in todo}
                for n, (layer, _, g, s, _) in enumerate(todo):
                    if n == 2 and c >= 2:
                        layer_out(2, c - 2, todo[0][3], turn)
                    if n == 6:
                        layer_out(1, c, ends[1], turn)
                        if c + 2 < CHUNKS:
                            copy_x(c + 2, turn)
                    if n == 7 and 0 in ends:
                        layer_out(0, c + 1, ends[0], turn)
                    if layer == 0:
                        round_layer0(c + 1, g, s, turn)
                    else:
                        round_pair(g, s, 2, turn)
                if c == 0:
                    layer_out(1, 0, ends[1], None)
                    copy_x(2, None)
                    layer_out(0, 1, ends[0], None)

            copy_x(0, None)
            act.wait_ge(small_here, 16 * SMALL)
            round_layer0(0, 0, 0, None)
            layer_out(0, 0, 2, None)
            copy_x(1, None)
            tops = [(wt1[:], w_top1[0:2 * P, :].rearrange("(k p) n -> p k n", p=P)), (wt1_dense[:], w_top1[2 * P:, :]),
                    (wt2[:], w_top2.rearrange("(k p) n -> p k n", p=P))]
            assert len(tops) == TOPS
            for dst, src in tops:
                act.dma_start(dst, src).then_inc(top_here, 16)
            all_iterations(act, iteration)
            act.wait_ge(sum2_made, CHUNKS - 1)
            layer_out(2, CHUNKS - 1, SPLITS * CHUNKS, None)

            act.wait_ge(top_here, 16 * TOPS)
            for m in range(4):
                act.wait_ge(top1_done, m + 1)
                nc.scalar.activation(hid1[:, m, :], top_bank[m][:], ACT.Relu, bias=bt1[:, m:m + 1]).then_inc(hid1_ready, 1)
            for m in range(2):
                act.wait_ge(top2_done, m + 1)
                nc.scalar.activation(hid2[:, m, :], (acc0, acc1)[m][:], ACT.Relu, bias=bt2[:, m:m + 1]).then_inc(hid2_ready, 1)

        @block.tensor
        def _(pe):
            def turn_x(c, turn):
                pe.wait_ge(gather_done[c % 2], at(16 * GATHERS * (c // 2 + 1), 8 * GATHERS, turn))
                if c:
                    pe.wait_ge(x_copied, at(c, 1, turn))
                nc.tensor.transpose(x_bank[:, 0:P], gathered[:, c % 2].rearrange("p j e -> p (j e)"),
                                    ident[:]).then_inc(x_turned, 1)

            pe.wait_ge(ident_here, 16)
            for u in range(W_LOTS):
                if u == 0:
                    pe.wait_ge(sym_made, 4)
                elif u == 2:
                    pe.wait_ge(w1_here, 16)
                elif u == 6:
                    pe.wait_ge(w2_here, 16)
                if u >= 2:
                    pe.wait_ge(w_ready, u - 1)
                if u < 2:
                    flat_sym = w_sym[:].rearrange("o j f i -> o (j f i)")
                    tiles = [flat_sym[:, t * P:(t + 1) * P] for t in (range(GROUP) if u == 0 else [GROUP])]
                else:
                    layer, k = divmod(u - 2, GROUPS)
                    tiles = [w_raw[layer][:, t * P:(t + 1) * P] for t in range(GROUP * k, GROUP * (k + 1))]
                for i, tile in enumerate(tiles):
                    op = nc.tensor.transpose(w_bank[u % 2][:, i * P:(i + 1) * P], tile, ident[:])
                op.then_inc(w_turned, 1)
            turn_x(0, None)
            pe.wait_ge(dense_here, 16)
            pe.wait_ge(w_ready, W_LOTS - 1)
            for i in range(BATCH // P):
                op = nc.tensor.transpose(w_bank[0][0:EMBED, i * P:(i + 1) * P], dense_rows[:, i, :], ident[:])
            op.then_inc(dense_turned, 1)

            def direct_pair(acc, w, zs, start=False):
                for i in range(2):
                    nc.tensor.matmul(acc[:], w[:, i], zs[:, i], start=start and i == 0, stop=False)

            def split_pair(acc, w_tile, s, start=False, stop=False):
                slot = s % PAIR_SLOTS
                for part, (w, zs) in enumerate(((w_high, z_high), (w_low, z_high), (w_high, z_low))):
                    for i in range(2):
                        op = nc.tensor.matmul(acc[:], w[:, w_tile + i], zs[:, slot, i],
                                              start=start and part == i == 0, stop=stop and part == 2 and i == 1)
                op.then_inc(pairs_used, 1)

            def layer0(chunk, s, turn):
                if chunk:
                    pe.wait_ge(kept0_out, at(chunk, 1, turn))
                for pair in range(2):
                    pe.wait_ge(low_dve, at(2 * chunk + pair + 1, 2, turn))
                    if pair == 1:
                        pe.wait_ge(last_parts, at(chunk + 1, 1, turn))
                        nc.tensor.matmul(acc0[:], wl_parts[:], zl_parts[:], start=False, stop=False)
                    split_pair(acc0, 2 * pair, s + pair, start=pair == 0, stop=pair == 1)

            def hidden(layer, chunk, k, g, s, p, turn):
                acc = acc1 if layer == 1 else acc2
                if k == 0 and chunk:
                    pe.wait_ge(kept1_out if layer == 1 else kept2_out, at(chunk, 1, turn))
                lot = GROUPS * (layer - 1) + k
                pe.wait_ge(z_made, at(g + 1, STEPS, turn))
                direct_pair(acc, w_direct[:, 2 * lot:2 * lot + 2], z[:, g % Z_SLOTS, 0:2], start=k == 0)
                pe.wait_ge(low_pool, at(p + 1, POOLED, turn))
                split_pair(acc, GROUP + 2 * lot, s, stop=k + 1 == GROUPS)

            def iteration(c, turn):
                for n, (layer, k, g, s, p) in enumerate(steps(c)):
                    if layer == 0:
                        layer0(c + 1, s, turn)
                    else:
                        hidden(layer, c + 1 - layer, k, g, s, p, turn)
                    if n == 3 and c + 2 < CHUNKS:
                        turn_x(c + 2, turn)
                    if n == 2 and c == CHUNKS:
                        top1_first()

            def top1_first():
                pe.wait_ge(top_here, 16 * TOPS)
                pe.wait_ge(dense_ready, 1)
                pe.wait_ge(sum01_made, CHUNKS)
                pe.wait_ge(x_copied, CHUNKS)
                for m in range(4):
                    cols = slice(m * P, (m + 1) * P)
                    nc.tensor.matmul(top_bank[m][:], wt1_dense[:, cols], dense_t[:], start=True, stop=False)
                    nc.tensor.matmul(top_bank[m][:], wt1[:, 0, cols], sum01[:], start=False, stop=False)

            pe.wait_ge(w_ready, W_LOTS)
            layer0(0, 0, None)
            turn_x(1, None)
            all_iterations(pe, iteration)
            pe.wait_ge(sum2_made, CHUNKS)
            for m in range(4):
                nc.tensor.matmul(top_bank[m][:], wt1[:, 1, m * P:(m + 1) * P], sum2[:],
                                 start=False, stop=True).then_inc(top1_done, 1)
            for k in range(4):
                pe.wait_ge(hid1_ready, k + 1)
                for m in range(2):
                    op = nc.tensor.matmul((acc0, acc1)[m][:], wt2[:, k, m * P:(m + 1) * P], hid1[:, k, :],
                                          start=k == 0, stop=k == 3)
                    if k == 3:
                        op.then_inc(top2_done, 1)
            for k in range(2):
                pe.wait_ge(hid2_ready, k + 1)
                op = nc.tensor.matmul(acc2[0:1, :], wt3[:, k:k + 1], hid2[:, k, :], start=k == 0, stop=k == 1)
            op.then_inc(top3_done, 1)


def kernel(**inputs):
    import concourse.bacc as bacc
    import numpy as np
    from concourse.bass_utils import run_bass_kernel_spmd

    tables = [np.asarray(inputs[f"tbl_{f}"]) for f in range(FIELDS)]
    first = np.concatenate([[0], np.cumsum([t.shape[0] for t in tables])[:-1]]).astype(np.int32)
    lay = lambda a: np.ascontiguousarray(
        a.reshape(CHUNKS, ROWS, P // ROWS, GATHERS).transpose(2, 1, 0, 3).reshape(P, CHUNKS * GATHERS))
    signs = np.zeros((P, 2), np.float32)
    signs[1::GROUP, 0] = -1.0
    signs[2::GROUP, 1] = -1.0
    arrays = {
        "idx": lay(np.asarray(inputs["ids"])),
        "row0": lay(np.broadcast_to(first, (BATCH, FIELDS))),
        "ident": np.eye(P, dtype=np.float32),
        "signs": signs,
        "table": np.concatenate(tables, axis=0),
        "dense_ctx": np.asarray(inputs["dense_ctx"]),
    }
    for i in range(3):
        arrays[f"W{i}"] = np.asarray(inputs[f"L0_rec_W{i}"])
    for name in ("W_top1", "W_top2"):
        arrays[name] = np.asarray(inputs[name])
    per_row = [inputs[name] for name in ("L0_rec_b0", "L0_rec_b1", "L0_rec_b2", "b_top1", "b_top2", "W_top3")]
    arrays["columns"] = np.concatenate([np.asarray(a).reshape(-1, P) for a in per_row], axis=0).T
    arrays = {f"in_{name}": np.ascontiguousarray(a) for name, a in arrays.items()}

    nc = bacc.Bacc("TRN2", target_bir_lowering=False, num_devices=1)
    ap = {name[3:]: nc.dram_tensor(name, a.shape, mybir.dt.from_np(a.dtype), kind="ExternalInput").ap()
          for name, a in arrays.items()}
    out = nc.dram_tensor("out", (BATCH, 1), F32, kind="ExternalOutput").ap()
    dlrm_tower(nc, ap["idx"], ap["row0"], ap["ident"], ap["signs"], ap["columns"], ap["table"], ap["dense_ctx"],
               [ap[f"W{i}"] for i in range(3)], ap["W_top1"], ap["W_top2"], out)
    return run_bass_kernel_spmd(nc, [arrays], core_ids=[0]).results[0]["out"]
```

```python
from contextlib import ExitStack
from dataclasses import dataclass

import concourse.bass as bass
from concourse import mybir

P = 128
FIELDS, EMBED, BATCH = 32, 16, 512
HALF = 64
ROWS = 32
CHUNKS = BATCH // ROWS
N = ROWS * EMBED
GATHERS = FIELDS * ROWS // P
GROUP = 4
TILES = FIELDS * HALF // P
GROUPS = TILES // GROUP
ROT = FIELDS // 2

Z_SLOTS, PAIR_SLOTS = 3, 5
W_LOTS = 2 + 2 * GROUPS
X_LOT = 4
SUM_AT = 3
X2_AT = 2
L0_AT = 2
X0_LOADS, SMALL, TOPS = GROUP + 2, 2, 3
GATHERS_FIRST = 6
GATHERS_AT = (0, 0, 0, 0, 3, 0, 1, 3, 1)
FIRST = 2
TURNS = (CHUNKS - 4 - FIRST + 1) // 2

F32 = mybir.dt.float32
F32R = mybir.dt.float32r
I32 = mybir.dt.int32
U32 = mybir.dt.uint32
ALU = mybir.AluOpType
ACT = mybir.ActivationFunctionType
AX = mybir.AxisListType

assert N == 512 and TILES == 16 and GROUPS == 4


@dataclass(frozen=True)
class Pair:

    layer: int
    chunk: int
    k: int
    i: int
    group: int
    by: str
    count: int
    split: int


@dataclass(frozen=True)
class Step:

    layer: int
    chunk: int
    k: int
    group: int
    pairs: tuple

    def by(self, *engines):
        return [pair for pair in self.pairs if pair.by in engines]


EXTRA = lambda c, layer, k: EX.get(c, EXC).get((layer, k), 'tensor')
EXC, EX, BV = {(2, 2): 'vector'}, {}, ((2, 2),)


def hands(c, layer, k):
    if layer == 0:
        return "vector", "vector"
    return EXTRA(c, layer, k), "vector" if (layer, k) in BV else "pool"


def plan():
    counts = {"group": 0, "tensor": 0, "vector": 0, "pool": 0, "split": 0}

    def step(c, layer, chunk, k):
        pairs = []
        for i, by in enumerate(hands(c, layer, k)):
            pairs.append(Pair(layer, chunk, k, i, counts["group"], by, counts[by], counts["split"]))
            counts[by] += 1
            counts["split"] += by != "tensor"
        counts["group"] += 1
        return Step(layer, chunk, k, pairs[0].group, tuple(pairs))

    start, iterations = step(-1, 0, 0, 0), []
    for c in range(CHUNKS + 1):
        layer1, layer0, layer2 = [[(layer, chunk, k) for k in range(GROUPS if layer else 1) if 0 <= chunk < CHUNKS]
                                  for layer, chunk in ((1, c), (0, c + 1), (2, c - 1))]
        order = layer1 + layer0 + layer2 if c else layer1[:L0_AT] + layer0 + layer1[L0_AT:]
        iterations.append([step(c, *of) for of in order])
    return start, iterations


def lateness():
    steps = [(c, step) for c, iteration in enumerate(PLAN) for step in iteration]
    due = [[] for _ in range(len(steps) + 1)]
    for place, (c, step) in enumerate(steps):
        for pair in step.by("vector", "pool"):
            due[place + (0 if c == 0 and step.layer == 0 else 1 if step.layer else 1 + pair.i)].append(pair)
    behind = [[sorted(due[place], key=lambda pair: pair.split) for place, (of, _) in enumerate(steps) if of == c]
              for c in range(len(PLAN))]
    return behind, due[-1]


START, PLAN = plan()
BEHIND, LEFT = lateness()
BY_GROUP = {step.group: step for steps in PLAN for step in steps} | {0: START}

ORDER = list(START.pairs)
for steps, behind in zip(PLAN, BEHIND):
    for step, pairs in zip(steps, behind):
        ORDER += step.by("tensor") + pairs
ORDER += LEFT
OPENS = {(pair.layer, pair.chunk): pair for pair in reversed(ORDER)}
CLOSES = {(pair.layer, pair.chunk): pair for pair in ORDER}

TURN = {by: sum(pair.by == by for steps in PLAN[FIRST:FIRST + 2] for step in steps for pair in step.pairs)
        for by in ("tensor", "vector", "pool")}
TURN["split"] = TURN["vector"] + TURN["pool"]
TURN["group"] = 2 * (2 * GROUPS + 1)

RUNS = -(-TURN["split"] // PAIR_SLOTS)
SLOT_ORDER = [slot for run in range(RUNS) for slot in range(TURN["split"] // RUNS + (run < TURN["split"] % RUNS))]


def slot_of(split):
    return SLOT_ORDER[(split - PLAN[FIRST][0].pairs[1].split) % TURN["split"]]


def last_in_slot(split):
    return max((other for other in range(split) if slot_of(other) == slot_of(split)), default=None)


assert TURN["group"] % Z_SLOTS == 0
for before, then in zip(PLAN[FIRST - 1][-Z_SLOTS:], PLAN[FIRST + 1][-Z_SLOTS:]):
    assert [pair.by for pair in before.pairs] == [pair.by for pair in then.pairs]
for n in range(2):
    begins, ends = PLAN[FIRST][0].pairs[n], PLAN[FIRST + 2 * TURNS][0].pairs[n]
    assert ends.split - begins.split == TURNS * TURN["split"] and ends.group - begins.group == TURNS * TURN["group"]


def split_weights(u):
    return (0, GROUP, 0) if u == 0 else (GROUP + 2 * (u - 2), 2, 2 * P)


def flat(tiles):
    return tiles.rearrange("p t o -> p (t o)")


def dlrm_tower(nc, idx_in, row0_in, ident_in, signs_in, columns_in, table, dense, w_cin, w_top1, w_top2, out):
    with ExitStack() as ctx:
        def sb(name, shape, dt=F32):
            return ctx.enter_context(nc.sbuf_tensor(name, shape, dt))

        def psum(name):
            return ctx.enter_context(nc.psum_tensor(name, [P, N], F32))

        def sem(name):
            return ctx.enter_context(nc.semaphore(name))

        x_dram = nc.dram_tensor("x_scratch", (2, 2 * FIELDS, N), F32, kind="Internal").ap()

        idx = sb("idx", [P, CHUNKS * GATHERS], I32)
        row0 = sb("row0", [P, CHUNKS * GATHERS], I32)
        rows_all = sb("rows_all", [P, CHUNKS * GATHERS], I32)
        rows_now = sb("rows_now", [P, 2, GATHERS], I32)
        ident = sb("ident", [P, P])
        signs = sb("signs", [P, 2])
        gathered = sb("gathered", [P, 2, GATHERS, EMBED])
        x_t = sb("x_t", [P, P])
        x_pair = sb("x_pair", [P, 2, TILES, N])
        x_rep = sb("x_rep", [P, N])
        x_rot = sb("x_rot", [P, GROUP, N])
        x_half = sb("x_half", [P, N])
        z = sb("z", [P, Z_SLOTS, GROUP, N])
        z_high = sb("z_high", [P, PAIR_SLOTS, 2, N], F32R)
        z_low = sb("z_low", [P, PAIR_SLOTS, 2, N], F32R)
        zl_full = sb("zl_full", [P, N])
        zl_high = sb("zl_high", [P, N], F32R)
        zl_parts = sb("zl_parts", [P, N], F32R)
        w_direct = sb("w_direct", [P, TILES, P])
        w_high = sb("w_high", [P, GROUP + TILES, P], F32R)
        w_low = sb("w_low", [P, GROUP + TILES, P], F32R)
        we_high = sb("we_high", [P, TILES, P], F32R)
        we_low = sb("we_low", [P, TILES, P], F32R)
        wl_high = sb("wl_high", [P, P], F32R)
        wl_parts = sb("wl_parts", [P, P], F32R)
        columns = sb("columns", [P, 11])
        bias, bt1, bt2, wt3 = columns[:, 0:3], columns[:, 3:7], columns[:, 7:9], columns[:, 9:11]
        kept01 = sb("kept01", [P, 2, N])
        kept2 = sb("kept2", [P, N])
        sum01 = sb("sum01", [P, BATCH])
        sum2 = sb("sum2", [P, BATCH])
        dense_rows = sb("dense_rows", [P, BATCH // P, EMBED])
        dense_t = sb("dense_t", [EMBED, BATCH])
        result = sb("result", [P, BATCH // P])

        hid1 = x_pair[:, 0, 0:4, :]
        hid2 = x_pair[:, 0, 4:6, :]
        wt1 = x_pair[:, 0, 6:8, :]
        wt1_dense = x_pair[0:EMBED, 0, 8, :]
        wt2 = flat(x_pair[:, 0, 9:11, :]).rearrange("p (k n) -> p k n", k=4)
        w_sym = flat(z[:, 1])[:, 0:(GROUP + 1) * P].rearrange("p (t f i) -> p t f i", t=GROUP + 1, f=FIELDS)
        w_raw = [x_pair[:, 1, 4 * i:4 * i + 4, :].rearrange("p t n -> p (t n)") for i in range(4)]
        w0_wide = w_raw[2].rearrange("p (f g) -> p f g", f=FIELDS)
        w0_tall = w_raw[3].rearrange("p (f g) -> p f g", g=FIELDS)

        acc0, acc1, acc2 = psum("acc0"), psum("acc1"), psum("acc2")
        h1 = psum("h1")
        h2 = [psum("h2_even"), psum("h2_odd")]
        x_bank = psum("x_bank")
        spare = psum("spare")
        w_bank = [spare, h2[1]]
        out_bank = [acc2, h1]
        top_bank = [h1, h2[0], x_bank, spare]

        idx_here, w0_here, w1_here, w2_here = sem("idx_here"), sem("w0_here"), sem("w1_here"), sem("w2_here")
        ident_here, small_here, top_here = sem("ident_here"), sem("small_here"), sem("top_here")
        wide_made = sem("wide_made")
        rows_made, rows_copied = sem("rows_made"), sem("rows_copied")
        sym_made, w_turned, w_rounded, w_ready = sem("sym_made"), sem("w_turned"), sem("w_rounded"), sem("w_ready")
        w_copied, extra_rounded, extra_ready = sem("w_copied"), sem("extra_rounded"), sem("extra_ready")
        dense_here, dense_turned, dense_ready = sem("dense_here"), sem("dense_turned"), sem("dense_ready")
        gather_done = [sem("gather_even"), sem("gather_odd")]
        x_turned, x_copied, x_stored, x0_here = sem("x_turned"), sem("x_copied"), sem("x_stored"), sem("x0_here")
        start_here = [sem(f"start_here_{j}") for j in range(GROUP + 1)]
        xp_here = [[sem(f"xp_here_{b}_{k}") for k in range(GROUPS)] for b in range(2)]
        start_made, z_made, last_made = sem("start_made"), sem("z_made"), sem("last_made")
        high_made, last_high = sem("high_made"), sem("last_high")
        low_dve, low_pool, last_parts = sem("low_dve"), sem("low_pool"), sem("last_parts")
        pairs_used, direct_used = sem("pairs_used"), sem("direct_used")
        h1_ready, h2_ready = sem("h1_ready"), sem("h2_ready")
        kept0_out, kept1_out, kept2_out = sem("kept0_out"), sem("kept1_out"), sem("kept2_out")
        sum01_made, sum2_made = sem("sum01_made"), sem("sum2_made")
        top1_done, hid1_ready = sem("top1_done"), sem("hid1_ready")
        top2_done, hid2_ready, top3_done = sem("top2_done"), sem("hid2_ready"), sem("top3_done")
        half_result = sem("half_result")
        result_ready, out_stored = sem("result_ready"), sem("out_stored")

        def acc_of(layer, chunk):
            return {(1, 0): spare, (2, CHUNKS - 1): acc1}.get((layer, chunk), (acc0, acc1, acc2)[layer])

        def at(first, per_iteration, turn):
            return first if turn is None else first + turn * (2 * per_iteration)

        def nth(first, kind, turn):
            return first if turn is None else first + turn * TURN[kind]

        def all_iterations(eng, iteration):
            for c in range(FIRST):
                iteration(c, None)
            with eng.Fori(0, TURNS) as turn:
                iteration(FIRST, turn)
                iteration(FIRST + 1, turn)
            for c in range(FIRST + 2 * TURNS, CHUNKS + 1):
                iteration(c, None)

        def products_of(pair):
            return z[:, pair.group % Z_SLOTS, 2 * pair.i:2 * pair.i + 2]

        block = ctx.enter_context(nc.Block())

        @block.sync
        def _(sp):
            sp.dma_start(idx[:], idx_in).then_inc(idx_here, 16)
            sp.dma_start(row0[:], row0_in).then_inc(idx_here, 16)
            w0 = w_cin[0].rearrange("o (f g) -> o f g", g=FIELDS)
            for half in range(2):
                sp.dma_start(w0_tall[:, half * FIELDS:(half + 1) * FIELDS, :], w0).then_inc(w0_here, 16)
            sp.dma_start(w_raw[0], w_cin[1]).then_inc(w1_here, 16)
            sp.dma_start(w_raw[1], w_cin[2]).then_inc(w2_here, 16)

            def store_x(c, turn):
                sp.wait_ge(x_copied, at(c + 1, 1, turn))
                for half in range(2):
                    rows = x_dram[c % 2, half * FIELDS:(half + 1) * FIELDS, :]
                    sp.dma_start(rows.rearrange("(q j) (e b) -> (j e) q b", j=GATHERS, b=ROWS),
                                 x_t[:].rearrange("p (q b) -> p q b", b=ROWS)).then_inc(x_stored, 16)

            def load_x0(c, turn):
                sp.wait_ge(x_stored, at(32 * (c + 1), 32, turn))
                x = x_dram[c % 2]
                wide = [FIELDS, GROUP, N]
                here = start_here if c == 0 else [x0_here] * (GROUP + 1)
                sp.dma_start(x_rep[:], x[0:FIELDS].unsqueeze(1).to_broadcast(wide)).then_inc(here[0], 16)
                for j in range(GROUP):
                    rotated = bass.AP(x.tensor, x.offset + GROUP * j * N, [[N, FIELDS], [N, GROUP], [1, N]])
                    sp.dma_start(x_rot[:, j, :], rotated).then_inc(here[j], 16)
                    if j == 1:
                        sp.dma_start(x_half[:], x[ROT:ROT + FIELDS].unsqueeze(1).to_broadcast(wide)).then_inc(here[GROUP], 16)

            def load_pair(c, k):
                src = x_dram[c % 2, 2 * GROUP * k:2 * GROUP * (k + 1), :].rearrange("(t a) n -> a t n", a=2)
                for a in range(2):
                    sp.dma_start(x_pair[HALF * a:HALF * (a + 1), c % 2, GROUP * k:GROUP * (k + 1), :],
                                 src[a:a + 1].to_broadcast([HALF, GROUP, N])).then_inc(xp_here[c % 2][k], 16)

            store_x(0, None)
            load_x0(0, None)
            for k in range(GROUPS):
                if k == L0_AT:
                    sp.wait_ge(start_made, GROUP)
                    load_x0(1, None)
                load_pair(0, k)
                if k == 0:
                    store_x(1, None)
            sp.wait_ge(w_turned, W_LOTS)
            for k in range(GROUPS):
                if k == X2_AT:
                    for here in xp_here[0]:
                        sp.wait_ge(here, 32)
                    store_x(2, None)
                load_pair(1, k)
            sp.wait_ge(last_made, 2)
            load_x0(2, None)

            def iteration(c, turn):
                used = {step.k: step.group for step in PLAN[c] if step.layer == 2}
                if c and c + 2 < CHUNKS:
                    store_x(c + 2, turn)
                for k in range(GROUPS):
                    if k == 2 and c and c + 2 < CHUNKS:
                        load_x0(c + 2, turn)
                    if c and c + 1 < CHUNKS:
                        sp.wait_ge(z_made, nth(used[k], "group", turn))
                        load_pair(c + 1, k)

            all_iterations(sp, iteration)
            sp.wait_ge(z_made, PLAN[CHUNKS - 1][-1].group)
            tops = [(wt1, w_top1[0:2 * P, :].rearrange("(k p) n -> p k n", p=P)), (wt1_dense, w_top1[2 * P:, :]),
                    (wt2, w_top2.rearrange("(k p) n -> p k n", p=P))]
            assert len(tops) == TOPS
            for dst, src in tops:
                sp.dma_start(dst, src).then_inc(top_here, 16)
            sp.wait_ge(result_ready, 1)
            sp.dma_start(out.rearrange("(p m) o -> p (m o)", p=P), result[:]).then_inc(out_stored, 16)
            sp.wait_ge(out_stored, 16)

        @block.gpsimd
        def _(pool):
            def copy_rows(c, turn):
                first = c * GATHERS if turn is None else turn * (2 * GATHERS) + c * GATHERS
                nc.gpsimd.tensor_copy(rows_now[:, c % 2, :],
                                      rows_all[:, bass.ds(first, GATHERS)]).then_inc(rows_copied, 1)
                pool.wait_ge(rows_copied, at(c + 1, 1, turn))

            def gather(c, j):
                pool.indirect_dma_start(
                    gathered[:, c % 2, j, :], None, table,
                    bass.IndirectOffsetOnAxis(ap=rows_now[:, c % 2, j:j + 1].bitcast(U32), axis=0),
                ).then_inc(gather_done[c % 2], 16)

            pool.wait_ge(rows_made, 1)
            for c in range(3):
                if c == 2:
                    pool.wait_ge(x_turned, 1)
                copy_rows(c, None)
                for j in range(GATHERS):
                    gather(c, j)

            def iteration(c, turn):
                gathers = 0
                if c + 3 < CHUNKS:
                    pool.wait_ge(x_turned, at(c + 2, 1, turn))
                    copy_rows(c + 3, turn)
                if c == 0:
                    gathers = GATHERS_FIRST
                    for j in range(gathers):
                        gather(3, j)
                for n, step in enumerate(PLAN[c]):
                    for pair in step.by("pool"):
                        pool.wait_ge(high_made, nth(pair.split + 1, "split", turn))
                        nc.gpsimd.tensor_tensor(z_low[:, slot_of(pair.split)], products_of(pair),
                                                z_high[:, slot_of(pair.split)].bitcast(F32),
                                                ALU.subtract).then_inc(low_pool, 1)
                    if c + 3 < CHUNKS:
                        upto = GATHERS if n + 1 == len(PLAN[c]) or c == 0 and n == 1 else gathers + GATHERS_AT[n] * (c > 0)
                        for j in range(gathers, upto):
                            gather(c + 3, j)
                        gathers = upto

            all_iterations(pool, iteration)

        @block.vector
        def _(dve):
            dve.wait_ge(idx_here, 32)
            nc.vector.tensor_tensor(rows_all[:], idx[:], row0[:], ALU.add).then_inc(rows_made, 1)

            def diagonals(raw, first, dims):
                return bass.AP(raw.tensor, raw.offset + first, [list(raw.ap[0])] + dims)

            wide, tall = 2 * FIELDS, FIELDS
            nc.vector.memset(w_sym[:, GROUP], 0.0).then_inc(sym_made, 1)
            dve.wait_ge(wide_made, 2)
            nc.vector.tensor_tensor(
                w_sym[:, 0:GROUP],
                diagonals(w0_wide, 0, [[GROUP, GROUP], [wide + 1, FIELDS], [1, GROUP]]),
                diagonals(w0_tall, 0, [[GROUP * tall, GROUP], [tall + 1, FIELDS], [tall, GROUP]]),
                ALU.add).then_inc(sym_made, 1)
            dve.wait_ge(sym_made, 2)
            nc.vector.tensor_copy(w_sym[:, 0, :, 0], diagonals(w0_wide, 0, [[wide + 1, FIELDS]])).then_inc(sym_made, 1)
            nc.vector.tensor_tensor(
                w_sym[:, GROUP, 0:ROT, 0:3],
                diagonals(w0_wide, ROT, [[wide + 1, ROT], [0, 3]]),
                diagonals(w0_tall, ROT * tall, [[tall + 1, ROT], [0, 3]]),
                ALU.add).then_inc(sym_made, 1)

            dve.wait_ge(small_here, 16 * SMALL)
            for u in range(W_LOTS):
                dve.wait_ge(w_rounded, u + 1)
                if u == 1:
                    op = nc.vector.scalar_tensor_tensor(out=wl_parts[:], in0=wl_high[:].bitcast(F32),
                                                        scalar=signs[:, 1:2], in1=w_bank[1][:, 0:P],
                                                        op0=ALU.mult, op1=ALU.add)
                else:
                    first, n, column = split_weights(u)
                    op = nc.vector.tensor_tensor(flat(w_low[:, first:first + n]), w_bank[u % 2][:, column:],
                                                 flat(w_high[:, first:first + n]).bitcast(F32), ALU.subtract)
                op.then_inc(w_ready, 1)
            dve.wait_ge(dense_turned, 1)
            nc.vector.tensor_copy(dense_t[:], w_bank[0][0:EMBED, :]).then_inc(dense_ready, 1)

            def free_slot(step, turn):
                if step.group < Z_SLOTS:
                    return
                last = BY_GROUP[step.group - Z_SLOTS]
                for by, left in (("tensor", direct_used), ("pool", low_pool), ("vector", low_dve)):
                    pairs = last.by(by)
                    if pairs:
                        dve.wait_ge(left, nth(pairs[-1].count + 1, by, turn))

            def products0(step, turn):
                dve.wait_ge(x0_here, at(X0_LOADS * 16 * step.chunk, X0_LOADS * 16, turn))
                nc.vector.tensor_tensor(z[:, step.group % Z_SLOTS], x_rep[:].unsqueeze(1).to_broadcast([P, GROUP, N]),
                                        x_rot[:], ALU.mult).then_inc(z_made, 1)
                nc.vector.tensor_tensor(zl_full[:], x_rep[:], x_half[:], ALU.mult).then_inc(last_made, 1)

            def products(step, turn):
                chunk, k = step.chunk, step.k
                if step.layer == 1:
                    dve.wait_ge(xp_here[chunk % 2][k], at(32 * (chunk // 2 + 1), 16, turn))
                if k == 0:
                    dve.wait_ge(h1_ready if step.layer == 1 else h2_ready, at(chunk + 1, 1, turn))
                h = h1 if step.layer == 1 else h2[chunk % 2]
                nc.vector.tensor_tensor(z[:, step.group % Z_SLOTS], h[:].unsqueeze(1).to_broadcast([P, GROUP, N]),
                                        x_pair[:, chunk % 2, GROUP * k:GROUP * (k + 1), :],
                                        ALU.mult).then_inc(z_made, 1)

            def low_part(pair, turn):
                dve.wait_ge(high_made, nth(pair.split + 1, "split", turn))
                nc.vector.tensor_tensor(z_low[:, slot_of(pair.split)], products_of(pair),
                                        z_high[:, slot_of(pair.split)].bitcast(F32), ALU.subtract).then_inc(low_dve, 1)
                if (pair.layer, pair.i) == (0, 1):
                    dve.wait_ge(last_high, at(pair.chunk + 1, 1, turn))
                    nc.vector.scalar_tensor_tensor(out=zl_parts[:], in0=zl_high[:].bitcast(F32),
                                                   scalar=signs[:, 0:1], in1=zl_full[:],
                                                   op0=ALU.mult, op1=ALU.add).then_inc(last_parts, 1)

            def sum_components(chunk, turn, kept, total, ready, made):
                dve.wait_ge(ready, at(chunk + 1, 1, turn))
                first = chunk * ROWS if turn is None else turn * (2 * ROWS) + chunk * ROWS
                nc.vector.tensor_reduce(total[:, bass.ds(first, ROWS)], kept.rearrange("p (e b) -> p b e", b=ROWS),
                                        AX.X, ALU.add).then_inc(made, 1)

            def iteration(c, turn):
                last = len(PLAN[c]) - 1
                for n, step in enumerate(PLAN[c]):
                    free_slot(step, turn)
                    (products if step.layer else products0)(step, turn)
                    for pair in BEHIND[c][n]:
                        if pair.by == "vector":
                            low_part(pair, turn)
                    if n == (SUM_AT if c == 1 else 1) and c >= 1:
                        sum_components(c - 1, turn, kept01[:, (c - 1) % 2], sum01, kept1_out, sum01_made)
                    if n == last and c >= 2:
                        sum_components(c - 2, turn, kept2[:], sum2, kept2_out, sum2_made)

            def start_products():
                for j in (0, 1, GROUP, 2, 3):
                    dve.wait_ge(start_here[j], 16 if j else 32)
                    if j == GROUP:
                        nc.vector.tensor_tensor(zl_full[:], x_rep[:], x_half[:], ALU.mult).then_inc(last_made, 1)
                    else:
                        nc.vector.tensor_tensor(z[:, 0, j], x_rep[:], x_rot[:, j, :], ALU.mult).then_inc(start_made, 1)

            start_products()
            for pair in START.pairs:
                low_part(pair, None)
            for half in range(2):
                dve.wait_ge(extra_rounded, half + 1)
                tiles = slice(half * TILES // 2, (half + 1) * TILES // 2)
                nc.vector.tensor_tensor(flat(we_low[:, tiles]), flat(w_direct[:, tiles]),
                                        flat(we_high[:, tiles]).bitcast(F32), ALU.subtract).then_inc(extra_ready, 1)
            all_iterations(dve, iteration)
            for pair in LEFT:
                if pair.by == "vector":
                    low_part(pair, None)
            sum_components(CHUNKS - 1, None, kept2[:], sum2, kept2_out, sum2_made)
            dve.wait_ge(top3_done, 1)
            nc.vector.tensor_copy(result[:], out_bank[0][:, 0:BATCH // P]).then_inc(half_result, 1)
            dve.wait_ge(half_result, 1)
            nc.vector.tensor_tensor(result[:], out_bank[1][:, 0:BATCH // P], result[:], ALU.add).then_inc(result_ready, 1)

        @block.scalar
        def _(act):
            act.dma_start(ident[:], ident_in).then_inc(ident_here, 16)
            smalls = [(signs[:], signs_in), (columns[:], columns_in)]
            assert len(smalls) == SMALL
            for dst, src in smalls:
                act.dma_start(dst, src).then_inc(small_here, 16)
            act.dma_start(dense_rows[:], dense.rearrange("(t p) e -> p t e", p=P)).then_inc(dense_here, 16)

            act.wait_ge(w0_here, 32)
            for half in range(2):
                nc.scalar.activation(w0_wide[:, :, half * FIELDS:(half + 1) * FIELDS], w0_tall[:, 0:FIELDS, :],
                                     ACT.Copy).then_inc(wide_made, 1)

            def copy_x(c, turn):
                act.wait_ge(x_turned, at(c + 1, 1, turn))
                if c:
                    act.wait_ge(x_stored, at(32 * c, 32, turn))
                nc.scalar.activation(x_t[:], x_bank[:, 0:P], ACT.Copy).then_inc(x_copied, 1)

            for u in range(W_LOTS):
                if u == X_LOT:
                    copy_x(0, None)
                act.wait_ge(w_turned, u + 1)
                if u == 1:
                    op = nc.scalar.activation(wl_high[:], w_bank[1][:, 0:P], ACT.Copy)
                else:
                    first, n, column = split_weights(u)
                    if column:
                        nc.scalar.activation(flat(w_direct[:, 2 * (u - 2):2 * (u - 1)]), w_bank[u % 2][:, 0:column],
                                             ACT.Copy).then_inc(w_copied, 1)
                    op = nc.scalar.activation(flat(w_high[:, first:first + n]), w_bank[u % 2][:, column:], ACT.Copy)
                op.then_inc(w_rounded, 1)

            def high_parts(step, turn):
                if step is not START:
                    act.wait_ge(z_made, nth(step.group, "group", turn))
                for pair in step.by("vector", "pool"):
                    if step is START:
                        act.wait_ge(start_made, 2 * (pair.i + 1))
                    last = last_in_slot(pair.split)
                    if last is not None:
                        act.wait_ge(pairs_used, nth(last + 1, "split", turn))
                    nc.scalar.activation(z_high[:, slot_of(pair.split)], products_of(pair), ACT.Copy).then_inc(high_made, 1)
                if step.layer == 0:
                    act.wait_ge(last_made, at(step.chunk + 1, 1, turn))
                    nc.scalar.activation(zl_high[:], zl_full[:], ACT.Copy).then_inc(last_high, 1)

            def relu(dst, acc, layer, half=None):
                rows = slice(None) if half is None else slice(HALF * half, HALF * (half + 1))
                return nc.scalar.activation(dst, acc[rows, :], ACT.Relu, bias=bias[rows, layer:layer + 1])

            def layer_out(layer, chunk, turn):
                act.wait_ge(pairs_used, nth(CLOSES[layer, chunk].split + 1, "split", turn))
                if layer == 2:
                    relu(kept2[:], acc_of(2, chunk), 2).then_inc(kept2_out, 1)
                    return
                acc = acc_of(layer, chunk)
                h, ready, out_sem = ((h1, h1_ready, kept0_out), (h2[chunk % 2], h2_ready, kept1_out))[layer]
                relu(h[0:HALF, :], acc, layer, 1)
                relu(h[HALF:P, :], acc, layer, 1).then_inc(ready, 1)
                relu(kept01[HALF * layer:HALF * (layer + 1), chunk % 2], acc, layer, 0).then_inc(out_sem, 1)

            def iteration(c, turn):
                for n, step in enumerate(PLAN[c]):
                    if n == 2 and c == 1:
                        layer_out(1, 0, None)
                    if n == 3 and c >= 2:
                        layer_out(2, c - 2, turn)
                    if n == 7:
                        layer_out(1, c, turn)
                    if n == 8:
                        layer_out(0, c + 1, turn)
                    high_parts(step, turn)
                    if c == 0 and step.layer == 0 or c and (step.layer, step.k) == (1, GROUPS - 1) and c + 2 < CHUNKS:
                        copy_x(c + 2, turn)
                if c == 0:
                    layer_out(0, 1, None)

            act.wait_ge(small_here, 16 * SMALL)
            copy_x(1, None)
            high_parts(START, None)
            for half in range(2):
                tiles = slice(half * TILES // 2, (half + 1) * TILES // 2)
                nc.scalar.activation(flat(we_high[:, tiles]), flat(w_direct[:, tiles]), ACT.Copy).then_inc(extra_rounded, 1)
            layer_out(0, 0, None)
            all_iterations(act, iteration)
            act.wait_ge(sum2_made, CHUNKS - 1)
            layer_out(2, CHUNKS - 1, None)

            act.wait_ge(top_here, 16 * TOPS)
            for m in range(4):
                act.wait_ge(top1_done, m + 1)
                nc.scalar.activation(hid1[:, m, :], top_bank[m][:], ACT.Relu, bias=bt1[:, m:m + 1]).then_inc(hid1_ready, 1)
            for m in range(2):
                act.wait_ge(top2_done, m + 1)
                nc.scalar.activation(hid2[:, m, :], (acc0, acc1)[m][:], ACT.Relu, bias=bt2[:, m:m + 1]).then_inc(hid2_ready, 1)

        @block.tensor
        def _(pe):
            def turn_x(c, turn):
                pe.wait_ge(gather_done[c % 2], at(16 * GATHERS * (c // 2 + 1), 8 * GATHERS, turn))
                if c:
                    pe.wait_ge(x_copied, at(c, 1, turn))
                nc.tensor.transpose(x_bank[:, 0:P], gathered[:, c % 2].rearrange("p j e -> p (j e)"),
                                    ident[:]).then_inc(x_turned, 1)

            pe.wait_ge(ident_here, 16)
            for u in range(W_LOTS):
                if u == X_LOT:
                    turn_x(0, None)
                if u == 0:
                    pe.wait_ge(sym_made, 4)
                elif u == 2:
                    pe.wait_ge(w1_here, 16)
                elif u == 6:
                    pe.wait_ge(w2_here, 16)
                if u >= 2:
                    pe.wait_ge(w_ready, u - 1)
                if u < 2:
                    flat_sym = w_sym.rearrange("o j f i -> o (j f i)")
                    tiles = [flat_sym[:, t * P:(t + 1) * P] for t in (range(GROUP) if u == 0 else [GROUP])]
                else:
                    layer, k = divmod(u - 2, GROUPS)
                    tiles = [w_raw[layer][:, t * P:(t + 1) * P] for t in range(GROUP * k, GROUP * (k + 1))]
                for i, tile in enumerate(tiles):
                    op = nc.tensor.transpose(w_bank[u % 2][:, i * P:(i + 1) * P], tile, ident[:])
                op.then_inc(w_turned, 1)
            pe.wait_ge(dense_here, 16)
            pe.wait_ge(w_ready, W_LOTS - 1)
            for i in range(BATCH // P):
                op = nc.tensor.transpose(w_bank[0][0:EMBED, i * P:(i + 1) * P], dense_rows[:, i, :], ident[:])
            op.then_inc(dense_turned, 1)


            def free_accumulator(pair, turn):
                if pair is OPENS[pair.layer, pair.chunk] and pair.chunk and (pair.layer, pair.chunk) != (1, 1):
                    if acc_of(pair.layer, pair.chunk) is acc1:
                        pe.wait_ge(kept1_out, at(pair.chunk + (pair.layer == 2), 1, turn))
                    else:
                        pe.wait_ge(kept0_out if pair.layer == 0 else kept2_out, at(pair.chunk, 1, turn))

            def unsplit(pair, turn):
                free_accumulator(pair, turn)
                pe.wait_ge(z_made, nth(pair.group, "group", turn))
                first = 2 * (GROUPS * (pair.layer - 1) + pair.k)
                for i in range(2):
                    op = nc.tensor.matmul(acc_of(pair.layer, pair.chunk)[:], w_direct[:, first + i], products_of(pair)[:, i],
                                          start=i == 0 and pair is OPENS[pair.layer, pair.chunk], stop=False)
                op.then_inc(direct_used, 1)

            def split(pair, turn):
                acc = acc_of(pair.layer, pair.chunk)
                free_accumulator(pair, turn)
                pe.wait_ge(low_dve if pair.by == "vector" else low_pool, nth(pair.count + 1, pair.by, turn))
                if (pair.layer, pair.i) == (0, 1):
                    pe.wait_ge(last_parts, at(pair.chunk + 1, 1, turn))
                    nc.tensor.matmul(acc[:], wl_parts[:], zl_parts[:], start=False, stop=False)
                first = 2 * pair.i if pair.layer == 0 else GROUP + 2 * (GROUPS * (pair.layer - 1) + pair.k)
                high, low = w_high, w_low
                if pair.layer and pair.i == 0:
                    high, low, first = we_high, we_low, first - GROUP
                slot = slot_of(pair.split)
                for part, (w, zs) in enumerate(((high, z_high), (low, z_high), (high, z_low))):
                    for i in range(2):
                        op = nc.tensor.matmul(acc[:], w[:, first + i], zs[:, slot, i],
                                              start=part == i == 0 and pair is OPENS[pair.layer, pair.chunk],
                                              stop=part == 2 and i == 1 and pair is CLOSES[pair.layer, pair.chunk])
                op.then_inc(pairs_used, 1)

            def iteration(c, turn):
                for n, step in enumerate(PLAN[c]):
                    for pair in step.by("tensor"):
                        unsplit(pair, turn)
                    for pair in BEHIND[c][n]:
                        split(pair, turn)
                    if n == 2 and c + 2 < CHUNKS:
                        turn_x(c + 2, turn)

            def top1_first():
                pe.wait_ge(top_here, 16 * TOPS)
                pe.wait_ge(dense_ready, 1)
                pe.wait_ge(sum01_made, CHUNKS)
                pe.wait_ge(x_copied, CHUNKS)
                for m in range(4):
                    cols = slice(m * P, (m + 1) * P)
                    nc.tensor.matmul(top_bank[m][:], wt1_dense[:, cols], dense_t[:], start=True, stop=False)
                    nc.tensor.matmul(top_bank[m][:], wt1[:, 0, cols], sum01[:], start=False, stop=False)

            pe.wait_ge(w_ready, W_LOTS)
            turn_x(1, None)
            for pair in START.pairs:
                split(pair, None)
            pe.wait_ge(extra_ready, 2)
            all_iterations(pe, iteration)
            for pair in LEFT:
                split(pair, None)
            top1_first()
            pe.wait_ge(sum2_made, CHUNKS)
            for m in range(4):
                nc.tensor.matmul(top_bank[m][:], wt1[:, 1, m * P:(m + 1) * P], sum2[:],
                                 start=False, stop=True).then_inc(top1_done, 1)
            for m in range(2):
                for k in range(4):
                    if m == 0:
                        pe.wait_ge(hid1_ready, k + 1)
                    op = nc.tensor.matmul((acc0, acc1)[m][:], wt2[:, k, m * P:(m + 1) * P], hid1[:, k, :],
                                          start=k == 0, stop=k == 3)
                op.then_inc(top2_done, 1)
            for k in range(2):
                pe.wait_ge(hid2_ready, k + 1)
                for m in range(4):
                    rows = hid2[:, k, :].rearrange("p (b m) -> p m b", m=4)[:, m, :]
                    op = nc.tensor.matmul(out_bank[k][:, m:m + 1], rows, wt3[:, k:k + 1], start=True, stop=True)
            op.then_inc(top3_done, 1)


def kernel(**inputs):
    import concourse.bacc as bacc
    import numpy as np
    from concourse.bass_utils import run_bass_kernel_spmd

    tables = [np.asarray(inputs[f"tbl_{f}"]) for f in range(FIELDS)]
    first = np.concatenate([[0], np.cumsum([t.shape[0] for t in tables])[:-1]]).astype(np.int32)
    lay = lambda a: np.ascontiguousarray(
        a.reshape(CHUNKS, ROWS, P // ROWS, GATHERS).transpose(2, 1, 0, 3).reshape(P, CHUNKS * GATHERS))
    signs = np.zeros((P, 2), np.float32)
    signs[1::GROUP, 0] = -1.0
    signs[2::GROUP, 1] = -1.0
    arrays = {
        "idx": lay(np.asarray(inputs["ids"])),
        "row0": lay(np.broadcast_to(first, (BATCH, FIELDS))),
        "ident": np.eye(P, dtype=np.float32),
        "signs": signs,
        "table": np.concatenate(tables, axis=0),
        "dense_ctx": np.asarray(inputs["dense_ctx"]),
    }
    for i in range(3):
        arrays[f"W{i}"] = np.asarray(inputs[f"L0_rec_W{i}"])
    for name in ("W_top1", "W_top2"):
        arrays[name] = np.asarray(inputs[name])
    per_row = [inputs[name] for name in ("L0_rec_b0", "L0_rec_b1", "L0_rec_b2", "b_top1", "b_top2", "W_top3")]
    arrays["columns"] = np.concatenate([np.asarray(a).reshape(-1, P) for a in per_row], axis=0).T
    arrays = {f"in_{name}": np.ascontiguousarray(a) for name, a in arrays.items()}

    nc = bacc.Bacc("TRN2", target_bir_lowering=False, num_devices=1)
    ap = {name[3:]: nc.dram_tensor(name, a.shape, mybir.dt.from_np(a.dtype), kind="ExternalInput").ap()
          for name, a in arrays.items()}
    out = nc.dram_tensor("out", (BATCH, 1), F32, kind="ExternalOutput").ap()
    dlrm_tower(nc, ap["idx"], ap["row0"], ap["ident"], ap["signs"], ap["columns"], ap["table"], ap["dense_ctx"],
               [ap[f"W{i}"] for i in range(3)], ap["W_top1"], ap["W_top2"], out)
    return run_bass_kernel_spmd(nc, [arrays], core_ids=[0]).results[0]["out"]
```

```python
from contextlib import ExitStack
from dataclasses import dataclass

import concourse.bass as bass
from concourse import mybir

P = 128
FIELDS, EMBED, BATCH = 32, 16, 512
HALF = 64
ROWS = 32
CHUNKS = BATCH // ROWS
N = ROWS * EMBED
GATHERS = FIELDS * ROWS // P
GROUP = 4
TILES = FIELDS * HALF // P
GROUPS = TILES // GROUP
ROT = FIELDS // 2
COPIES = 3

Z_SLOTS, PAIR_SLOTS = 3, 5
X0_LOADS, SMALL, TOPS = GROUP + 1, 2, COPIES + 2
W_LOTS = 2 + 2 * GROUPS
X_LOT = 4
L0_AT = 2
X2_AT = 2
BUSY = 12
FIRST = 2
TURNS = (CHUNKS - 4 - FIRST + 1) // 2
AHEAD = 3
GATHERED = ((6, 8, 8, 8, 8), (0, 0, 0, 0, 3, 3, 4, 7, 8))

F32 = mybir.dt.float32
F32R = mybir.dt.float32r
I32 = mybir.dt.int32
U32 = mybir.dt.uint32
ALU = mybir.AluOpType
ACT = mybir.ActivationFunctionType
AX = mybir.AxisListType

assert N == 512 and TILES == 16 and GROUPS == 4


@dataclass(frozen=True)
class Pair:

    layer: int
    chunk: int
    k: int
    i: int
    group: int
    by: str
    count: int
    split: int


@dataclass(frozen=True)
class Step:

    layer: int
    chunk: int
    k: int
    group: int
    pairs: tuple

    def by(self, *engines):
        return [pair for pair in self.pairs if pair.by in engines]


HANDS = {0: "tp tp tp tp  pp tp vv tp", 1: "tp tp tp tp  tp tp vv tp",
         13: "tp tp tp tp  pp tp pp tp", 14: "tp tp tp tp  pp tp pp tp", 15: "tp pv tp pv  tp pv tp pv"}
ENGINES = {"t": "tensor", "v": "vector", "p": "pool"}


def hands(c, layer, k):
    if layer == 0:
        return "vector", "vector"
    return [ENGINES[by] for by in HANDS.get(c, HANDS[c % 2]).split()[GROUPS * (layer - 1) + k]]


def plan():
    counts = {"group": 0, "tensor": 0, "vector": 0, "pool": 0, "split": 0}

    def step(c, layer, chunk, k):
        pairs = []
        for i, by in enumerate(hands(c, layer, k)):
            pairs.append(Pair(layer, chunk, k, i, counts["group"], by, counts[by], counts["split"]))
            counts[by] += 1
            counts["split"] += by != "tensor"
        counts["group"] += 1
        return Step(layer, chunk, k, pairs[0].group, tuple(pairs))

    start, iterations = step(-1, 0, 0, 0), []
    for c in range(CHUNKS + 1):
        layer1, layer0, layer2 = [[(layer, chunk, k) for k in range(GROUPS if layer else 1) if 0 <= chunk < CHUNKS]
                                  for layer, chunk in ((1, c), (0, c + 1), (2, c - 1))]
        order = layer1 + layer0 + layer2 if c else layer1[:L0_AT] + layer0 + layer1[L0_AT:]
        iterations.append([step(c, *of) for of in order])
    return start, iterations


def lateness():
    steps = [(c, step) for c, iteration in enumerate(PLAN) for step in iteration]
    due = [[] for _ in range(len(steps) + 1)]
    for place, (c, step) in enumerate(steps):
        for pair in step.by("vector", "pool"):
            due[place + (0 if c == 0 and step.layer == 0 else 1 if step.layer else 1 + pair.i)].append(pair)
    behind = [[sorted(due[place], key=lambda pair: pair.split) for place, (of, _) in enumerate(steps) if of == c]
              for c in range(len(PLAN))]
    return behind, due[-1]


START, PLAN = plan()
BEHIND, LEFT = lateness()
AWAITED = (PLAN[0][0], PLAN[1][0])
BY_GROUP = {step.group: step for steps in PLAN for step in steps} | {0: START}

ORDER = list(START.pairs)
for steps, behind in zip(PLAN, BEHIND):
    for step, pairs in zip(steps, behind):
        ORDER += step.by("tensor") + pairs
ORDER += LEFT
OPENS = {(pair.layer, pair.chunk): pair for pair in reversed(ORDER)}
CLOSES = {(pair.layer, pair.chunk): pair for pair in ORDER}

TURN = {by: sum(pair.by == by for steps in PLAN[FIRST:FIRST + 2] for step in steps for pair in step.pairs)
        for by in ("tensor", "vector", "pool")}
TURN["split"] = TURN["vector"] + TURN["pool"]
TURN["group"] = 2 * (2 * GROUPS + 1)

RUNS = -(-TURN["split"] // PAIR_SLOTS)
SLOT_ORDER = [slot for run in range(RUNS) for slot in range(TURN["split"] // RUNS + (run < TURN["split"] % RUNS))]


def squares_behind(c):
    return next((step for step in PLAN[c] if c + 1 < CHUNKS and (step.layer == 0 if c == 0 else step.k == GROUPS - 1)),
                None)


def slot_of(split):
    return SLOT_ORDER[(split - PLAN[FIRST][0].pairs[1].split) % TURN["split"]]


def last_in_slot(split):
    return max((other for other in range(split) if slot_of(other) == slot_of(split)), default=None)


assert TURN["group"] % Z_SLOTS == 0
for before, then in zip(PLAN[FIRST - 1][-Z_SLOTS:], PLAN[FIRST + 1][-Z_SLOTS:]):
    assert [pair.by for pair in before.pairs] == [pair.by for pair in then.pairs]
for n in range(2):
    begins, ends = PLAN[FIRST][0].pairs[n], PLAN[FIRST + 2 * TURNS][0].pairs[n]
    assert ends.split - begins.split == TURNS * TURN["split"] and ends.group - begins.group == TURNS * TURN["group"]


def split_weights(u):
    return (0, GROUP, 0) if u == 0 else (GROUP + 2 * (u - 2), 2, 2 * P)


def flat(tiles):
    return tiles.rearrange("p t o -> p (t o)")


def dlrm_tower(nc, idx_in, row0_in, ident_in, signs_in, columns_in, table, dense, w_cin, w_top1, w_top2, out):
    with ExitStack() as ctx:
        def sb(name, shape, dt=F32):
            return ctx.enter_context(nc.sbuf_tensor(name, shape, dt))

        def psum(name):
            return ctx.enter_context(nc.psum_tensor(name, [P, N], F32))

        def sem(name):
            return ctx.enter_context(nc.semaphore(name))

        x_dram = nc.dram_tensor("x_scratch", (2, 2 * FIELDS, N), F32, kind="Internal").ap()

        idx = sb("idx", [P, CHUNKS * GATHERS], I32)
        row0 = sb("row0", [P, CHUNKS * GATHERS], I32)
        rows_all = sb("rows_all", [P, CHUNKS * GATHERS], I32)
        rows_now = sb("rows_now", [P, 2, GATHERS], I32)
        ident = sb("ident", [P, P])
        signs = sb("signs", [P, 4])
        gathered = sb("gathered", [P, 2, GATHERS, EMBED])
        x_t = sb("x_t", [P, P])
        x_pair = sb("x_pair", [P, 2, TILES, N])
        x_rep = sb("x_rep", [P, N])
        x_rot = sb("x_rot", [P, GROUP, N])
        z = sb("z", [P, Z_SLOTS, GROUP, N])
        z_high = sb("z_high", [P, PAIR_SLOTS, 2, N], F32R)
        z_low = sb("z_low", [P, PAIR_SLOTS, 2, N], F32R)
        zl_full = sb("zl_full", [P, N])
        zl_high = sb("zl_high", [P, N], F32R)
        zl_parts = sb("zl_parts", [P, N], F32R)
        w_direct = sb("w_direct", [P, TILES, P])
        wf_high = sb("wf_high", [P, TILES, P], F32R)
        wf_low = sb("wf_low", [P, TILES, P], F32R)
        w_high = sb("w_high", [P, GROUP + TILES, P], F32R)
        w_low = sb("w_low", [P, GROUP + TILES, P], F32R)
        wl_high = sb("wl_high", [P, P], F32R)
        wl_parts = sb("wl_parts", [P, P], F32R)
        columns = sb("columns", [P, 11])
        bias, bt1, bt2, wt3 = columns[:, 0:3], columns[:, 3:7], columns[:, 7:9], columns[:, 9:11]
        kept01 = sb("kept01", [P, 2, N])
        kept2 = sb("kept2", [P, N])
        sum01 = sb("sum01", [P, BATCH])
        sum2 = sb("sum2", [P, BATCH])
        dense_rows = sb("dense_rows", [P, BATCH // P, COPIES, EMBED])
        dense_high = sb("dense_high", [COPIES * EMBED, BATCH], F32R)
        dense_parts = sb("dense_parts", [COPIES * EMBED, BATCH], F32R)
        result = sb("result", [P, BATCH // P])

        hid1 = x_pair[:, 0, 0:4, :]
        hid2 = x_pair[:, 0, 4:6, :]
        wt1 = x_pair[:, 0, 6:8, :]
        wt2 = flat(x_pair[:, 0, 8:10, :])
        wd = x_pair[0:COPIES * EMBED, 0, 10, :]
        wt1_high, wt1_low = [flat(w[:, 0:8]).rearrange("p (k n) -> p k n", k=2) for w in (w_high, w_low)]
        wd_high, wd_parts = [flat(w[0:COPIES * EMBED, 8:12]) for w in (w_high, w_low)]
        wt2_high, wt2_low = flat(wf_high[:, 0:8]), flat(wf_low[:, 0:8])
        sum01_high, sum01_low = zl_high[:], zl_parts[:]
        sum2_high, sum2_low = z_high[:, 0, 0], z_low[:, 0, 0]
        hid1_high, hid1_low = [parts[:, 1:3].rearrange("p s i n -> p (s i) n") for parts in (z_high, z_low)]
        w_sym = flat(z[:, 1])[:, 0:(GROUP + 1) * P].rearrange("p (t f i) -> p t f i", t=GROUP + 1, f=FIELDS)
        w_raw = [x_pair[:, 1, 4 * i:4 * i + 4, :].rearrange("p t n -> p (t n)") for i in range(4)]
        w0_wide = w_raw[2].rearrange("p (f g) -> p f g", f=FIELDS)
        w0_tall = w_raw[3].rearrange("p (f g) -> p f g", g=FIELDS)

        acc0, acc1, acc2 = psum("acc0"), psum("acc1"), psum("acc2")
        h1 = psum("h1")
        h2 = [psum("h2_even"), psum("h2_odd")]
        x_bank = psum("x_bank")
        spare = psum("spare")
        w_bank = [spare, h2[1]]
        dense_bank = h2[0]
        out_bank = [acc2, h1]
        top_bank = [h1, h2[0], x_bank, spare]

        idx_here, w0_here, w1_here, w2_here = sem("idx_here"), sem("w0_here"), sem("w1_here"), sem("w2_here")
        ident_here, small_here, top_here = sem("ident_here"), sem("small_here"), sem("top_here")
        wide_made = sem("wide_made")
        rows_made, rows_copied = sem("rows_made"), sem("rows_copied")
        sym_made, w_turned, w_rounded, w_ready = sem("sym_made"), sem("w_turned"), sem("w_rounded"), sem("w_ready")
        w_copied, first_rounded, first_split = sem("w_copied"), sem("first_rounded"), sem("first_split")
        dense_rounded = sem("dense_rounded")
        dense_here, dense_turned, dense_ready = sem("dense_here"), sem("dense_turned"), sem("dense_ready")
        gather_done = [sem("gather_even"), sem("gather_odd")]
        x_turned, x_copied, x_stored, x0_here = sem("x_turned"), sem("x_copied"), sem("x_stored"), sem("x0_here")
        start_here = [sem(f"start_here_{j}") for j in range(GROUP + 1)]
        xp_here = [[sem(f"xp_here_{b}_{k}") for k in range(GROUPS)] for b in range(2)]
        start_made, z_made, last_made = sem("start_made"), sem("z_made"), sem("last_made")
        high_made, last_high = sem("high_made"), sem("last_high")
        low_dve, low_pool, last_parts = sem("low_dve"), sem("low_pool"), sem("last_parts")
        pairs_used, direct_used = sem("pairs_used"), sem("direct_used")
        h1_ready, h2_ready = sem("h1_ready"), sem("h2_ready")
        kept0_out, kept1_out, kept2_out = sem("kept0_out"), sem("kept1_out"), sem("kept2_out")
        sum01_made, sum2_made = sem("sum01_made"), sem("sum2_made")
        top1_done, hid1_ready = sem("top1_done"), sem("hid1_ready")
        top2_done, hid2_ready, top3_done = sem("top2_done"), sem("hid2_ready"), sem("top3_done")
        half_result = sem("half_result")
        top_rounded, top_split, sum_rounded, sum_split = (sem("top_rounded"), sem("top_split"), sem("sum_rounded"),
                                                          sem("sum_split"))
        first_made = sem("first_made")
        first_stored = sem("first_stored")
        hid1_made, hid1_rounded = sem("hid1_made"), sem("hid1_rounded")
        result_ready, out_stored = sem("result_ready"), sem("out_stored")

        def acc_of(layer, chunk):
            return {(1, 0): spare, (2, CHUNKS - 1): acc1}.get((layer, chunk), (acc0, acc1, acc2)[layer])

        def at(first, per_iteration, turn):
            return first if turn is None else first + turn * (2 * per_iteration)

        def nth(first, kind, turn):
            return first if turn is None else first + turn * TURN[kind]

        def all_iterations(eng, iteration):
            for c in range(FIRST):
                iteration(c, None)
            with eng.Fori(0, TURNS) as turn:
                iteration(FIRST, turn)
                iteration(FIRST + 1, turn)
            for c in range(FIRST + 2 * TURNS, CHUNKS + 1):
                iteration(c, None)

        def products_of(pair):
            return z[:, pair.group % Z_SLOTS, 2 * pair.i:2 * pair.i + 2]

        block = ctx.enter_context(nc.Block())

        @block.sync
        def _(sp):
            sp.dma_start(idx[:], idx_in).then_inc(idx_here, 16)
            sp.dma_start(row0[:], row0_in).then_inc(idx_here, 16)
            w0 = w_cin[0].rearrange("o (f g) -> o f g", g=FIELDS)
            for half in range(2):
                sp.dma_start(w0_tall[:, half * FIELDS:(half + 1) * FIELDS, :], w0).then_inc(w0_here, 16)
            sp.dma_start(w_raw[0], w_cin[1]).then_inc(w1_here, 16)
            sp.dma_start(w_raw[1], w_cin[2]).then_inc(w2_here, 16)

            def store_x(c, turn):
                sp.wait_ge(x_copied, at(c + 1, 1, turn))
                for half in range(2):
                    rows = x_dram[c % 2, half * FIELDS:(half + 1) * FIELDS, :]
                    sp.dma_start(rows.rearrange("(q j) (e b) -> (j e) q b", j=GATHERS, b=ROWS),
                                 x_t[:].rearrange("p (q b) -> p q b", b=ROWS)).then_inc(
                                     first_stored if c == half == 0 else x_stored, 16)

            def load_x0(c, turn):
                if c == 0:
                    sp.wait_ge(first_stored, 16)
                else:
                    sp.wait_ge(x_stored, at(32 * c + 16, 32, turn))
                x = x_dram[c % 2]
                wide = [FIELDS, GROUP, N]
                here = start_here if c == 0 else [x0_here] * X0_LOADS
                sp.dma_start(x_rep[:], x[0:FIELDS].unsqueeze(1).to_broadcast(wide)).then_inc(here[0], 16)
                if c == 0:
                    sp.wait_ge(x_stored, 16)
                for j in range(GROUP):
                    rotated = bass.AP(x.tensor, x.offset + (1 + GROUP * j) * N, [[N, FIELDS], [N, GROUP], [1, N]])
                    sp.dma_start(x_rot[:, j, :], rotated).then_inc(here[1 + j], 16)

            def load_pair(c, k):
                src = x_dram[c % 2, 2 * GROUP * k:2 * GROUP * (k + 1), :].rearrange("(t a) n -> a t n", a=2)
                for a in range(2):
                    sp.dma_start(x_pair[HALF * a:HALF * (a + 1), c % 2, GROUP * k:GROUP * (k + 1), :],
                                 src[a:a + 1].to_broadcast([HALF, GROUP, N])).then_inc(xp_here[c % 2][k], 16)

            store_x(0, None)
            load_x0(0, None)
            for k in range(GROUPS):
                if k == L0_AT:
                    sp.wait_ge(start_made, GROUP)
                    sp.wait_ge(last_made, 1)
                    load_x0(1, None)
                load_pair(0, k)
                if k == 0:
                    store_x(1, None)
            sp.wait_ge(w_turned, W_LOTS)
            for k in range(GROUPS):
                if k == X2_AT:
                    for here in xp_here[0]:
                        sp.wait_ge(here, 32)
                    store_x(2, None)
                load_pair(1, k)
            sp.wait_ge(z_made, PLAN[0][L0_AT].group)
            sp.wait_ge(last_made, 2)
            load_x0(2, None)

            def iteration(c, turn):
                used = {step.k: step.group for step in PLAN[c] if step.layer == 2}
                if c and c + 2 < CHUNKS:
                    store_x(c + 2, turn)
                for k in range(GROUPS):
                    if k == GROUPS // 2 and c and c + 2 < CHUNKS:
                        load_x0(c + 2, turn)
                    if c and c + 1 < CHUNKS:
                        sp.wait_ge(z_made, nth(used[k], "group", turn))
                        load_pair(c + 1, k)

            all_iterations(sp, iteration)
            sp.wait_ge(z_made, PLAN[CHUNKS - 1][-1].group)
            tops = [(wd[EMBED * i:EMBED * (i + 1)], w_top1[2 * P:, :]) for i in range(COPIES)] + [
                (wt1, w_top1[0:2 * P, :].rearrange("(k p) n -> p k n", p=P)),
                (wt2.rearrange("p (k n) -> p k n", k=4), w_top2.rearrange("(k p) n -> p k n", p=P))]
            assert len(tops) == TOPS
            for dst, src in tops:
                sp.dma_start(dst, src).then_inc(top_here, 16)
            sp.wait_ge(result_ready, 1)
            sp.dma_start(out.rearrange("(p m) o -> p (m o)", p=P), result[:]).then_inc(out_stored, 16)
            sp.wait_ge(out_stored, 16)

        @block.gpsimd
        def _(pool):
            def copy_rows(c, turn):
                first = c * GATHERS if turn is None else turn * (2 * GATHERS) + c * GATHERS
                nc.gpsimd.tensor_copy(rows_now[:, c % 2, :],
                                      rows_all[:, bass.ds(first, GATHERS)]).then_inc(rows_copied, 1)
                pool.wait_ge(rows_copied, at(c - AHEAD + 1, 1, turn))

            def gather(c, j):
                rows = rows_all[:, c * GATHERS + j:c * GATHERS + j + 1] if c < AHEAD else rows_now[:, c % 2, j:j + 1]
                pool.indirect_dma_start(
                    gathered[:, c % 2, j, :], None, table, bass.IndirectOffsetOnAxis(ap=rows.bitcast(U32), axis=0),
                ).then_inc(gather_done[c % 2], 16)

            pool.wait_ge(rows_made, 1)
            for c in range(AHEAD):
                if c == 2:
                    pool.wait_ge(x_turned, 1)
                for j in range(GATHERS):
                    gather(c, j)

            def iteration(c, turn):
                gathers = 0
                if c + AHEAD < CHUNKS:
                    pool.wait_ge(x_turned, at(c + 2, 1, turn))
                    copy_rows(c + AHEAD, turn)
                if c == 0:
                    gathers = GATHERED[0][0]
                    for j in range(gathers):
                        gather(AHEAD, j)
                for n, step in enumerate(PLAN[c]):
                    for pair in step.by("pool"):
                        pool.wait_ge(high_made, nth(pair.split + 1, "split", turn))
                        nc.gpsimd.tensor_tensor(z_low[:, slot_of(pair.split)], products_of(pair),
                                                z_high[:, slot_of(pair.split)].bitcast(F32),
                                                ALU.subtract).then_inc(low_pool, 1)
                    if c + AHEAD < CHUNKS:
                        upto = GATHERED[c > 0][n]
                        for j in range(gathers, upto):
                            gather(c + AHEAD, j)
                        gathers = upto

            all_iterations(pool, iteration)

        @block.vector
        def _(dve):
            dve.wait_ge(idx_here, 32)
            nc.vector.tensor_tensor(rows_all[:], idx[:], row0[:], ALU.add).then_inc(rows_made, 1)

            def diagonals(raw, first, dims):
                return bass.AP(raw.tensor, raw.offset + first, [list(raw.ap[0])] + dims)

            wide, tall = 2 * FIELDS, FIELDS
            nc.vector.memset(w_sym[:, GROUP], 0.0).then_inc(sym_made, 1)
            dve.wait_ge(wide_made, 2)
            nc.vector.tensor_tensor(
                w_sym[:, 0:GROUP],
                diagonals(w0_wide, 1, [[GROUP, GROUP], [wide + 1, FIELDS], [1, GROUP]]),
                diagonals(w0_tall, tall, [[GROUP * tall, GROUP], [tall + 1, FIELDS], [tall, GROUP]]),
                ALU.add).then_inc(sym_made, 1)
            dve.wait_ge(sym_made, 2)
            nc.vector.tensor_copy(w_sym[:, GROUP - 1, :, GROUP - 1],
                                  diagonals(w0_wide, ROT, [[wide + 1, FIELDS]])).then_inc(sym_made, 1)
            nc.vector.tensor_copy(w_sym[:, GROUP, :, 0:3],
                                  diagonals(w0_wide, 0, [[wide + 1, FIELDS], [0, 3]])).then_inc(sym_made, 1)

            dve.wait_ge(small_here, 16 * SMALL)
            for u in range(W_LOTS):
                dve.wait_ge(w_rounded, u + 1)
                if u == 1:
                    op = nc.vector.scalar_tensor_tensor(out=wl_parts[:], in0=wl_high[:].bitcast(F32),
                                                        scalar=signs[:, 1:2], in1=w_bank[1][:, 0:P],
                                                        op0=ALU.mult, op1=ALU.add)
                else:
                    first, n, column = split_weights(u)
                    op = nc.vector.tensor_tensor(flat(w_low[:, first:first + n]), w_bank[u % 2][:, column:],
                                                 flat(w_high[:, first:first + n]).bitcast(F32), ALU.subtract)
                op.then_inc(w_ready, 1)

            def free_slot(step, turn):
                if step.group < Z_SLOTS:
                    return
                last = BY_GROUP[step.group - Z_SLOTS]
                for by, left in (("tensor", direct_used), ("pool", low_pool), ("vector", low_dve)):
                    pairs = last.by(by)
                    if pairs:
                        dve.wait_ge(left, nth(pairs[-1].count + 1, by, turn))

            def products0(step, turn):
                dve.wait_ge(x0_here, at(X0_LOADS * 16 * step.chunk, X0_LOADS * 16, turn))
                nc.vector.tensor_tensor(z[:, step.group % Z_SLOTS], x_rep[:].unsqueeze(1).to_broadcast([P, GROUP, N]),
                                        x_rot[:], ALU.mult).then_inc(z_made, 1)

            def products(step, turn):
                chunk, k = step.chunk, step.k
                if step.layer == 1:
                    dve.wait_ge(xp_here[chunk % 2][k], at(32 * (chunk // 2 + 1), 16, turn))
                if k == 0:
                    dve.wait_ge(h1_ready if step.layer == 1 else h2_ready, at(chunk + 1, 1, turn))
                h = h1 if step.layer == 1 else h2[chunk % 2]
                runs = ((0, 2), (2, 4)) if step in AWAITED else ((0, 4),)
                for first, end in runs:
                    nc.vector.tensor_tensor(z[:, step.group % Z_SLOTS, first:end],
                                            h[:].unsqueeze(1).to_broadcast([P, end - first, N]),
                                            x_pair[:, chunk % 2, GROUP * k + first:GROUP * k + end, :],
                                            ALU.mult).then_inc(z_made if end == GROUP else first_made, 1)

            def low_part(pair, turn):
                dve.wait_ge(high_made, nth(pair.split + 1, "split", turn))
                nc.vector.tensor_tensor(z_low[:, slot_of(pair.split)], products_of(pair),
                                        z_high[:, slot_of(pair.split)].bitcast(F32), ALU.subtract).then_inc(low_dve, 1)
                if (pair.layer, pair.i) == (0, 1):
                    dve.wait_ge(last_high, at(pair.chunk + 1, 1, turn))
                    nc.vector.scalar_tensor_tensor(out=zl_parts[:], in0=zl_high[:].bitcast(F32),
                                                   scalar=signs[:, 0:1], in1=zl_full[:],
                                                   op0=ALU.mult, op1=ALU.add).then_inc(last_parts, 1)

            def sum_components(chunk, turn, kept, total, ready, made):
                dve.wait_ge(ready, at(chunk + 1, 1, turn))
                first = chunk * ROWS if turn is None else turn * (2 * ROWS) + chunk * ROWS
                nc.vector.tensor_reduce(total[:, bass.ds(first, ROWS)], kept.rearrange("p (e b) -> p b e", b=ROWS),
                                        AX.X, ALU.add).then_inc(made, 1)

            def iteration(c, turn):
                last = len(PLAN[c]) - 1
                for n, step in enumerate(PLAN[c]):
                    free_slot(step, turn)
                    (products if step.layer else products0)(step, turn)
                    for pair in BEHIND[c][n]:
                        if pair.by == "vector":
                            low_part(pair, turn)
                    if n == (3 if c == 1 else 1) and c >= 1:
                        sum_components(c - 1, turn, kept01[:, (c - 1) % 2], sum01, kept1_out, sum01_made)
                    if n == last and c >= 2:
                        sum_components(c - 2, turn, kept2[:], sum2, kept2_out, sum2_made)

            def start_products():
                dve.wait_ge(start_here[0], 16)
                for j in range(GROUP):
                    dve.wait_ge(start_here[1 + j], 16)
                    nc.vector.tensor_tensor(z[:, 0, j], x_rep[:], x_rot[:, j, :], ALU.mult).then_inc(start_made, 1)

            start_products()
            for pair in START.pairs:
                low_part(pair, None)
            for half in range(2):
                dve.wait_ge(first_rounded, half + 1)
                tiles = slice(half * TILES // 2, (half + 1) * TILES // 2)
                nc.vector.tensor_tensor(flat(wf_low[:, tiles]), flat(w_direct[:, tiles]),
                                        flat(wf_high[:, tiles]).bitcast(F32), ALU.subtract).then_inc(first_split, 1)
            dve.wait_ge(dense_rounded, 1)
            nc.vector.scalar_tensor_tensor(out=dense_parts[:], in0=dense_high[:].bitcast(F32),
                                           scalar=signs[0:COPIES * EMBED, 2:3], in1=dense_bank[0:COPIES * EMBED, :],
                                           op0=ALU.mult, op1=ALU.add).then_inc(dense_ready, 1)
            all_iterations(dve, iteration)
            for pair in LEFT:
                if pair.by == "vector":
                    low_part(pair, None)

            def split_top(rounded, count, full, high, low, done):
                dve.wait_ge(rounded, count)
                nc.vector.tensor_tensor(low, full, high.bitcast(F32), ALU.subtract).then_inc(done, 1)

            dve.wait_ge(top_rounded, 1)
            nc.vector.scalar_tensor_tensor(out=wd_parts, in0=wd_high.bitcast(F32), scalar=signs[0:COPIES * EMBED, 3:4],
                                           in1=wd, op0=ALU.mult, op1=ALU.add).then_inc(top_split, 1)
            split_top(top_rounded, 2, wt1, wt1_high, wt1_low, top_split)
            split_top(sum_rounded, 1, sum01[:], sum01_high, sum01_low, top_split)
            split_top(top_rounded, 3, wt2, wt2_high, wt2_low, top_split)
            sum_components(CHUNKS - 1, None, kept2[:], sum2, kept2_out, sum2_made)
            split_top(sum_rounded, 2, sum2[:], sum2_high, sum2_low, sum_split)
            for m in range(4):
                split_top(hid1_rounded, m + 1, hid1[:, m, :], hid1_high[:, m, :], hid1_low[:, m, :], hid1_ready)
            dve.wait_ge(top3_done, 1)
            nc.vector.tensor_copy(result[:], out_bank[0][:, 0:BATCH // P]).then_inc(half_result, 1)
            dve.wait_ge(half_result, 1)
            nc.vector.tensor_tensor(result[:], out_bank[1][:, 0:BATCH // P], result[:],
                                    ALU.add).then_inc(result_ready, 1)

        @block.scalar
        def _(act):
            act.dma_start(ident[:], ident_in).then_inc(ident_here, 16)
            smalls = [(signs[:], signs_in), (columns[:], columns_in)]
            assert len(smalls) == SMALL
            for dst, src in smalls:
                act.dma_start(dst, src).then_inc(small_here, 16)
            for i in range(COPIES):
                act.dma_start(dense_rows[:, :, i, :], dense.rearrange("(t p) e -> p t e", p=P)).then_inc(dense_here, 16)

            act.wait_ge(w0_here, 32)
            for half in range(2):
                nc.scalar.activation(w0_wide[:, :, half * FIELDS:(half + 1) * FIELDS], w0_tall[:, 0:FIELDS, :],
                                     ACT.Copy).then_inc(wide_made, 1)

            def copy_x(c, turn):
                act.wait_ge(x_turned, at(c + 1, 1, turn))
                if c:
                    act.wait_ge(x_stored, at(32 * c - 16, 32, turn))
                if c == 1:
                    act.wait_ge(first_stored, 16)
                nc.scalar.activation(x_t[:], x_bank[:, 0:P], ACT.Copy).then_inc(x_copied, 1)

            for u in range(W_LOTS):
                if u == X_LOT:
                    copy_x(0, None)
                act.wait_ge(w_turned, u + 1)
                if u == 1:
                    op = nc.scalar.activation(wl_high[:], w_bank[1][:, 0:P], ACT.Copy)
                else:
                    first, n, column = split_weights(u)
                    if column:
                        nc.scalar.activation(flat(w_direct[:, 2 * (u - 2):2 * (u - 1)]), w_bank[u % 2][:, 0:column],
                                             ACT.Copy).then_inc(w_copied, 1)
                    op = nc.scalar.activation(flat(w_high[:, first:first + n]), w_bank[u % 2][:, column:], ACT.Copy)
                op.then_inc(w_rounded, 1)

            def high_parts(step, turn):
                if step is not START:
                    act.wait_ge(z_made, nth(step.group, "group", turn))
                for pair in step.by("vector", "pool"):
                    if step is START:
                        act.wait_ge(start_made, 2 * (pair.i + 1))
                    last = last_in_slot(pair.split)
                    if last is not None:
                        act.wait_ge(pairs_used, nth(last + 1, "split", turn))
                    nc.scalar.activation(z_high[:, slot_of(pair.split)], products_of(pair),
                                         ACT.Copy).then_inc(high_made, 1)
                    if pair is START.pairs[1]:
                        squares(0, None)

            def squares(chunk, turn):
                if chunk:
                    act.wait_ge(x0_here, at(X0_LOADS * 16 * chunk, X0_LOADS * 16, turn))
                    act.wait_ge(last_parts, at(chunk, 1, turn))
                else:
                    act.wait_ge(start_here[0], 16)
                nc.scalar.activation(zl_full[:], x_rep[:], ACT.Square).then_inc(last_made, 1)
                act.wait_ge(last_made, at(chunk + 1, 1, turn))
                nc.scalar.activation(zl_high[:], zl_full[:], ACT.Copy).then_inc(last_high, 1)

            def relu(dst, acc, layer, half=None):
                rows = slice(None) if half is None else slice(HALF * half, HALF * (half + 1))
                return nc.scalar.activation(dst, acc[rows, :], ACT.Relu, bias=bias[rows, layer:layer + 1])

            def layer_out(layer, chunk, turn):
                act.wait_ge(pairs_used, nth(CLOSES[layer, chunk].split + 1, "split", turn))
                if layer == 2:
                    relu(kept2[:], acc_of(2, chunk), 2).then_inc(kept2_out, 1)
                    return
                acc = acc_of(layer, chunk)
                h, ready, out_sem = ((h1, h1_ready, kept0_out), (h2[chunk % 2], h2_ready, kept1_out))[layer]
                relu(h[0:HALF, :], acc, layer, 1)
                relu(h[HALF:P, :], acc, layer, 1).then_inc(ready, 1)
                relu(kept01[HALF * layer:HALF * (layer + 1), chunk % 2], acc, layer, 0).then_inc(out_sem, 1)

            def iteration(c, turn):
                for n, step in enumerate(PLAN[c]):
                    if n == 2 and c == 1:
                        layer_out(1, 0, None)
                    if n == 3 and c >= 2:
                        layer_out(2, c - 2, turn)
                    if n == 7:
                        layer_out(1, c, turn)
                    if n == 8:
                        layer_out(0, c + 1, turn)
                    high_parts(step, turn)
                    if step is squares_behind(c):
                        squares(c + 1, turn)
                        if c + 2 < CHUNKS:
                            copy_x(c + 2, turn)
                if c == 0:
                    layer_out(0, 1, None)

            act.wait_ge(small_here, 16 * SMALL)
            copy_x(1, None)
            high_parts(START, None)
            for half in range(2):
                tiles = slice(half * TILES // 2, (half + 1) * TILES // 2)
                nc.scalar.activation(flat(wf_high[:, tiles]), flat(w_direct[:, tiles]),
                                     ACT.Copy).then_inc(first_rounded, 1)
            act.wait_ge(dense_turned, 1)
            nc.scalar.activation(dense_high[:], dense_bank[0:COPIES * EMBED, :], ACT.Copy).then_inc(dense_rounded, 1)
            layer_out(0, 0, None)
            all_iterations(act, iteration)
            act.wait_ge(top_here, 16 * TOPS)
            for high, full in ((wd_high, wd), (wt1_high, wt1), (wt2_high, wt2)):
                nc.scalar.activation(high, full, ACT.Copy).then_inc(top_rounded, 1)
            act.wait_ge(sum01_made, CHUNKS)
            nc.scalar.activation(sum01_high, sum01[:], ACT.Copy).then_inc(sum_rounded, 1)
            act.wait_ge(sum2_made, CHUNKS - 1)
            layer_out(2, CHUNKS - 1, None)
            act.wait_ge(sum2_made, CHUNKS)
            nc.scalar.activation(sum2_high, sum2[:], ACT.Copy).then_inc(sum_rounded, 1)

            for m in range(4):
                act.wait_ge(top1_done, m + 1)
                nc.scalar.activation(hid1[:, m, :], top_bank[m][:], ACT.Relu,
                                     bias=bt1[:, m:m + 1]).then_inc(hid1_made, 1)
                act.wait_ge(hid1_made, m + 1)
                nc.scalar.activation(hid1_high[:, m, :], hid1[:, m, :], ACT.Copy).then_inc(hid1_rounded, 1)
            for m in range(2):
                act.wait_ge(top2_done, m + 1)
                nc.scalar.activation(hid2[:, m, :], (acc0, acc1)[m][:], ACT.Relu,
                                     bias=bt2[:, m:m + 1]).then_inc(hid2_ready, 1)

        @block.tensor
        def _(pe):
            def turn_x(c, turn):
                pe.wait_ge(gather_done[c % 2], at(16 * GATHERS * (c // 2 + 1), 8 * GATHERS, turn))
                if c:
                    pe.wait_ge(x_copied, at(c, 1, turn))
                nc.tensor.transpose(x_bank[:, 0:P], gathered[:, c % 2].rearrange("p j e -> p (j e)"),
                                    ident[:]).then_inc(x_turned, 1)

            pe.wait_ge(ident_here, 16)
            for u in range(W_LOTS):
                if u == X_LOT:
                    turn_x(0, None)
                if u == 0:
                    pe.wait_ge(sym_made, 4)
                elif u == 2:
                    pe.wait_ge(w1_here, 16)
                elif u == 6:
                    pe.wait_ge(w2_here, 16)
                if u >= 2:
                    pe.wait_ge(w_ready, u - 1)
                if u < 2:
                    flat_sym = w_sym.rearrange("o j f i -> o (j f i)")
                    tiles = [flat_sym[:, t * P:(t + 1) * P] for t in (range(GROUP) if u == 0 else [GROUP])]
                else:
                    layer, k = divmod(u - 2, GROUPS)
                    tiles = [w_raw[layer][:, t * P:(t + 1) * P] for t in range(GROUP * k, GROUP * (k + 1))]
                for i, tile in enumerate(tiles):
                    op = nc.tensor.transpose(w_bank[u % 2][:, i * P:(i + 1) * P], tile, ident[:])
                op.then_inc(w_turned, 1)
            pe.wait_ge(dense_here, 16 * COPIES)
            for i in range(BATCH // P):
                op = nc.tensor.transpose(dense_bank[0:COPIES * EMBED, i * P:(i + 1) * P],
                                         dense_rows[:, i].rearrange("p c e -> p (c e)"), ident[:])
            op.then_inc(dense_turned, 1)

            def free_accumulator(pair, turn):
                if pair is OPENS[pair.layer, pair.chunk] and pair.chunk and (pair.layer, pair.chunk) != (1, 1):
                    if acc_of(pair.layer, pair.chunk) is acc1:
                        pe.wait_ge(kept1_out, at(pair.chunk + (pair.layer == 2), 1, turn))
                    else:
                        pe.wait_ge(kept0_out if pair.layer == 0 else kept2_out, at(pair.chunk, 1, turn))

            def unsplit(pair, turn):
                free_accumulator(pair, turn)
                if BY_GROUP[pair.group] in AWAITED:
                    pe.wait_ge(first_made, 1 + (pair.chunk == 1))
                else:
                    pe.wait_ge(z_made, nth(pair.group, "group", turn))
                first = 2 * (GROUPS * (pair.layer - 1) + pair.k)
                acc = acc_of(pair.layer, pair.chunk)
                for i in range(2):
                    op = nc.tensor.matmul(acc[:], w_direct[:, first + i], products_of(pair)[:, i],
                                          start=i == 0 and pair is OPENS[pair.layer, pair.chunk], stop=False)
                op.then_inc(direct_used, 1)

            def split(pair, turn):
                acc = acc_of(pair.layer, pair.chunk)
                free_accumulator(pair, turn)
                pe.wait_ge(low_dve if pair.by == "vector" else low_pool, nth(pair.count + 1, pair.by, turn))
                if (pair.layer, pair.i) == (0, 1):
                    pe.wait_ge(last_parts, at(pair.chunk + 1, 1, turn))
                    nc.tensor.matmul(acc[:], wl_parts[:], zl_parts[:], start=False, stop=False)
                first = 2 * pair.i if pair.layer == 0 else GROUP + 2 * (GROUPS * (pair.layer - 1) + pair.k)
                high, low = w_high, w_low
                if pair.layer and pair.i == 0:
                    high, low, first = wf_high, wf_low, first - GROUP
                slot = slot_of(pair.split)
                for part, (w, zs) in enumerate(((high, z_high), (low, z_high), (high, z_low))):
                    for i in range(2):
                        op = nc.tensor.matmul(acc[:], w[:, first + i], zs[:, slot, i],
                                              start=part == i == 0 and pair is OPENS[pair.layer, pair.chunk],
                                              stop=part == 2 and i == 1 and pair is CLOSES[pair.layer, pair.chunk])
                op.then_inc(pairs_used, 1)

            def iteration(c, turn):
                for n, step in enumerate(PLAN[c]):
                    for pair in step.by("tensor"):
                        unsplit(pair, turn)
                    for pair in BEHIND[c][n]:
                        split(pair, turn)
                    if n == 2 and c + 2 < CHUNKS:
                        turn_x(c + 2, turn)

            def three_products(bank, w, cols, x, start, stop):
                for n, (i, j) in enumerate(((0, 0), (1, 0), (0, 1))):
                    op = nc.tensor.matmul(bank[:], w[i][:, cols], x[j], start=start and n == 0, stop=stop and n == 2)
                return op

            def top1_first():
                pe.wait_ge(dense_ready, 1)
                pe.wait_ge(top_split, 3)
                for m in range(4):
                    cols = slice(m * P, (m + 1) * P)
                    nc.tensor.matmul(top_bank[m][:], wd_parts[:, cols], dense_parts[:], start=True, stop=False)
                    three_products(top_bank[m], (wt1_high[:, 0], wt1_low[:, 0]), cols, (sum01_high, sum01_low),
                                   False, False)

            pe.wait_ge(w_ready, W_LOTS)
            turn_x(1, None)
            for _ in range(BUSY):
                nc.tensor.transpose(acc2[:, 0:P], ident[:], ident[:])
            for pair in START.pairs:
                split(pair, None)
            pe.wait_ge(first_split, 2)
            all_iterations(pe, iteration)
            for pair in LEFT:
                split(pair, None)
            top1_first()
            pe.wait_ge(sum_split, 1)
            for m in range(4):
                three_products(top_bank[m], (wt1_high[:, 1], wt1_low[:, 1]), slice(m * P, (m + 1) * P),
                               (sum2_high, sum2_low), False, True).then_inc(top1_done, 1)
            pe.wait_ge(top_split, 4)
            for k in range(4):
                pe.wait_ge(hid1_ready, k + 1)
                for m in range(2):
                    first = k * 2 * P + m * P
                    op = three_products((acc0, acc1)[m], (wt2_high, wt2_low), slice(first, first + P),
                                        (hid1_high[:, k, :], hid1_low[:, k, :]), k == 0, k == 3)
                    if k == 3:
                        op.then_inc(top2_done, 1)
            for k in range(2):
                pe.wait_ge(hid2_ready, k + 1)
                for m in range(4):
                    rows = hid2[:, k, :].rearrange("p (b m) -> p m b", m=4)[:, m, :]
                    op = nc.tensor.matmul(out_bank[k][:, m:m + 1], rows, wt3[:, k:k + 1], start=True, stop=True)
            op.then_inc(top3_done, 1)


def kernel(**inputs):
    import concourse.bacc as bacc
    import numpy as np
    from concourse.bass_utils import run_bass_kernel_spmd

    tables = [np.asarray(inputs[f"tbl_{f}"]) for f in range(FIELDS)]
    first = np.concatenate([[0], np.cumsum([t.shape[0] for t in tables])[:-1]]).astype(np.int32)
    lay = lambda a: np.ascontiguousarray(
        a.reshape(CHUNKS, ROWS, P // ROWS, GATHERS).transpose(2, 1, 0, 3).reshape(P, CHUNKS * GATHERS))
    signs = np.zeros((P, 4), np.float32)
    signs[1::GROUP, 0] = -1.0
    signs[2::GROUP, 1] = -1.0
    signs[2 * EMBED:COPIES * EMBED, 2] = -1.0
    signs[1 * EMBED:2 * EMBED, 3] = -1.0
    arrays = {
        "idx": lay(np.asarray(inputs["ids"])),
        "row0": lay(np.broadcast_to(first, (BATCH, FIELDS))),
        "ident": np.eye(P, dtype=np.float32),
        "signs": signs,
        "table": np.concatenate(tables, axis=0),
        "dense_ctx": np.asarray(inputs["dense_ctx"]),
    }
    for i in range(3):
        arrays[f"W{i}"] = np.asarray(inputs[f"L0_rec_W{i}"])
    for name in ("W_top1", "W_top2"):
        arrays[name] = np.asarray(inputs[name])
    per_row = [inputs[name] for name in ("L0_rec_b0", "L0_rec_b1", "L0_rec_b2", "b_top1", "b_top2", "W_top3")]
    arrays["columns"] = np.concatenate([np.asarray(a).reshape(-1, P) for a in per_row], axis=0).T
    arrays = {f"in_{name}": np.ascontiguousarray(a) for name, a in arrays.items()}

    nc = bacc.Bacc("TRN2", target_bir_lowering=False, num_devices=1)
    ap = {name[3:]: nc.dram_tensor(name, a.shape, mybir.dt.from_np(a.dtype), kind="ExternalInput").ap()
          for name, a in arrays.items()}
    out = nc.dram_tensor("out", (BATCH, 1), F32, kind="ExternalOutput").ap()
    dlrm_tower(nc, ap["idx"], ap["row0"], ap["ident"], ap["signs"], ap["columns"], ap["table"], ap["dense_ctx"],
               [ap[f"W{i}"] for i in range(3)], ap["W_top1"], ap["W_top2"], out)
    return run_bass_kernel_spmd(nc, [arrays], core_ids=[0]).results[0]["out"]
```
